# Optimizing a Trainium2 kernel written in Bass

```python
import numpy as np
import jax
import jax.numpy as jnp

def _softmax(x, axis=-1):
    return jax.nn.softmax(x, axis=axis)

def _gelu(x):
    return jax.nn.gelu(x, approximate=True)

def _silu(x):
    return jax.nn.silu(x)

def _sigmoid(x):
    return jax.nn.sigmoid(x)

def _layernorm(x, axis=-1, eps=1e-05):
    m = jnp.mean(x, axis=axis, keepdims=True)
    v = jnp.var(x, axis=axis, keepdims=True)
    return (x - m) / jnp.sqrt(v + eps)

def _scatter_add(tgt, idx, src, axis=0):
    return tgt.at[idx].add(src)

def _segment_sum(src, seg, n):
    return jax.ops.segment_sum(src, seg, n)
kernel_name = 'mk_conv_seq_d4_conv_nhwc512_r4_6b8c22'

def setup_inputs(seed: int=0):
    np.random.seed(seed)
    _w = jnp.asarray

    def _rec_inputs():
        import jax
        import jax.numpy as jnp
        _gk = jax.random.key(seed)
        x = -0.0003929 + 0.9999 * jax.random.normal(jax.random.fold_in(_gk, 1), (8, 16, 16, 128), jnp.float32)
        return x
    x = _rec_inputs()

    def _L0_conv_setup():
        import jax, jax.numpy as jnp
        import numpy as np
        GROUPS = 16
        EPS = 0.001

        def group_norm(x, gamma, beta):
            B, H, W, C = x.shape
            xg = x.reshape(B, H, W, GROUPS, C // GROUPS)
            mean = jnp.mean(xg, axis=(1, 2, 4), keepdims=True)
            var = jnp.var(xg, axis=(1, 2, 4), keepdims=True)
            xn = (xg - mean) * jax.lax.rsqrt(var + EPS)
            xn = xn.reshape(B, H, W, C)
            return xn * gamma + beta
        key = jax.random.key(seed)
        ks = jax.random.split(key, 4)
        B, H, W, C = (8, 16, 16, 128)
        std = 0.05
        return {'x': jax.random.normal(ks[0], (B, H, W, C), dtype=jnp.float32), 'gn_gamma': jnp.ones((C,), dtype=jnp.float32), 'gn_beta': jnp.zeros((C,), dtype=jnp.float32), 'wq': jax.random.normal(ks[1], (C, C), dtype=jnp.float32) * std, 'bq': jnp.zeros((C,), dtype=jnp.float32), 'wk': jax.random.normal(ks[2], (C, C), dtype=jnp.float32) * std, 'bk': jnp.zeros((C,), dtype=jnp.float32), 'wv': jax.random.normal(ks[3], (C, C), dtype=jnp.float32) * std, 'bv': jnp.zeros((C,), dtype=jnp.float32)}
    _L0_conv_all = _L0_conv_setup()
    _L0_conv_in = {k: v for k, v in _L0_conv_all.items() if k in ('gn_gamma', 'gn_beta', 'wq', 'bq', 'wk', 'bk', 'wv', 'bv')}
    del _L0_conv_all

    def _L1_conv_setup():
        import jax, jax.numpy as jnp
        import numpy as np
        B, H, W, C = (32, 16, 16, 128)
        C8 = C // 8
        key = jax.random.key(seed)
        ks = jax.random.split(key, 5)
        scale = 1.0 / np.sqrt(C)
        x = jax.random.normal(ks[0], (B, H, W, C), dtype=jnp.float32)
        Wq = jax.random.normal(ks[1], (C, C8), dtype=jnp.float32) * scale
        Wk = jax.random.normal(ks[2], (C, C8), dtype=jnp.float32) * scale
        Wv = jax.random.normal(ks[3], (C, C), dtype=jnp.float32) * scale
        bq = jnp.zeros((C8,), dtype=jnp.float32)
        bk = jnp.zeros((C8,), dtype=jnp.float32)
        bv = jnp.zeros((C,), dtype=jnp.float32)
        gamma = jax.random.uniform(ks[4], (1,), dtype=jnp.float32)
        return {'x': x, 'Wq': Wq, 'bq': bq, 'Wk': Wk, 'bk': bk, 'Wv': Wv, 'bv': bv, 'gamma': gamma}
    _L1_conv_all = _L1_conv_setup()
    _L1_conv_in = {k: v for k, v in _L1_conv_all.items() if k in ('Wq', 'bq', 'Wk', 'bk', 'Wv', 'bv', 'gamma')}
    del _L1_conv_all

    def _L2_conv_setup():
        import jax, jax.numpy as jnp
        import numpy as np
        H, W = (21, 28)
        key = jax.random.key(seed)
        k1, k2, k3, k4, k5 = jax.random.split(key, 5)
        C = 128
        x = jax.random.normal(k1, (1, H, W, C), dtype=jnp.float32)
        Wb = jax.random.normal(k2, (C, C // 8), dtype=jnp.float32) * (2.0 / C) ** 0.5
        Wc = jax.random.normal(k3, (C, C // 8), dtype=jnp.float32) * (2.0 / C) ** 0.5
        Wd = jax.random.normal(k4, (C, C), dtype=jnp.float32) * (2.0 / C) ** 0.5
        gamma = jax.random.normal(k5, (1,), dtype=jnp.float32)
        return {'x': x, 'Wb': Wb, 'Wc': Wc, 'Wd': Wd, 'gamma': gamma}
    _L2_conv_all = _L2_conv_setup()
    _L2_conv_in = {k: v for k, v in _L2_conv_all.items() if k in ('Wb', 'Wc', 'Wd', 'gamma')}
    del _L2_conv_all

    def _L3_conv_setup():
        import jax, jax.numpy as jnp
        import numpy as np
        from jax import lax
        N_HEADS = 8
        D_K = 16
        D_V = 16
        TEMP = float(np.sqrt(D_K))

        def avg_pool_3x3_s2_same(x):
            sums = lax.reduce_window(x, 0.0, lax.add, (1, 3, 3, 1), (1, 2, 2, 1), 'SAME')
            ones = jnp.ones(x.shape[:3] + (1,), x.dtype)
            cnt = lax.reduce_window(ones, 0.0, lax.add, (1, 3, 3, 1), (1, 2, 2, 1), 'SAME')
            return sums / cnt

        def conv1x1(x, w, b):
            return jnp.einsum('bhwc,cd->bhwd', x, w) + b
        key = jax.random.key(seed)
        ks = jax.random.split(key, 6)
        C = 128
        s1 = float(np.sqrt(2.0 / (C + D_K)))
        s3 = float(np.sqrt(2.0 / (C + D_V)))
        return {'x': jax.random.normal(ks[0], (4, 16, 16, C), jnp.float32), 'w_q': jax.random.normal(ks[1], (C, N_HEADS * D_K), jnp.float32) * s1, 'b_q': jnp.zeros((N_HEADS * D_K,), jnp.float32), 'w_k': jax.random.normal(ks[2], (C, N_HEADS * D_K), jnp.float32) * s1, 'b_k': jnp.zeros((N_HEADS * D_K,), jnp.float32), 'w_v': jax.random.normal(ks[3], (C, N_HEADS * D_V), jnp.float32) * s3, 'b_v': jnp.zeros((N_HEADS * D_V,), jnp.float32), 'w_o': jax.random.normal(ks[4], (N_HEADS * D_V, C), jnp.float32) * 0.02, 'b_o': jnp.zeros((C,), jnp.float32)}
    _L3_conv_all = _L3_conv_setup()
    _L3_conv_in = {k: v for k, v in _L3_conv_all.items() if k in ('w_q', 'b_q', 'w_k', 'b_k', 'w_v', 'b_v', 'w_o', 'b_o')}
    del _L3_conv_all
    return {'x': x, 'L0_conv_gn_gamma': _L0_conv_in['gn_gamma'], 'L0_conv_gn_beta': _L0_conv_in['gn_beta'], 'L0_conv_wq': _L0_conv_in['wq'], 'L0_conv_bq': _L0_conv_in['bq'], 'L0_conv_wk': _L0_conv_in['wk'], 'L0_conv_bk': _L0_conv_in['bk'], 'L0_conv_wv': _L0_conv_in['wv'], 'L0_conv_bv': _L0_conv_in['bv'], 'L1_conv_Wq': _L1_conv_in['Wq'], 'L1_conv_bq': _L1_conv_in['bq'], 'L1_conv_Wk': _L1_conv_in['Wk'], 'L1_conv_bk': _L1_conv_in['bk'], 'L1_conv_Wv': _L1_conv_in['Wv'], 'L1_conv_bv': _L1_conv_in['bv'], 'L1_conv_gamma': _L1_conv_in['gamma'], 'L2_conv_Wb': _L2_conv_in['Wb'], 'L2_conv_Wc': _L2_conv_in['Wc'], 'L2_conv_Wd': _L2_conv_in['Wd'], 'L2_conv_gamma': _L2_conv_in['gamma'], 'L3_conv_w_q': _L3_conv_in['w_q'], 'L3_conv_b_q': _L3_conv_in['b_q'], 'L3_conv_w_k': _L3_conv_in['w_k'], 'L3_conv_b_k': _L3_conv_in['b_k'], 'L3_conv_w_v': _L3_conv_in['w_v'], 'L3_conv_b_v': _L3_conv_in['b_v'], 'L3_conv_w_o': _L3_conv_in['w_o'], 'L3_conv_b_o': _L3_conv_in['b_o']}

def reference(x, L0_conv_gn_gamma, L0_conv_gn_beta, L0_conv_wq, L0_conv_bq, L0_conv_wk, L0_conv_bk, L0_conv_wv, L0_conv_bv, L1_conv_Wq, L1_conv_bq, L1_conv_Wk, L1_conv_bk, L1_conv_Wv, L1_conv_bv, L1_conv_gamma, L2_conv_Wb, L2_conv_Wc, L2_conv_Wd, L2_conv_gamma, L3_conv_w_q, L3_conv_b_q, L3_conv_w_k, L3_conv_b_k, L3_conv_w_v, L3_conv_b_v, L3_conv_w_o, L3_conv_b_o):
    import jax
    import jax.numpy as jnp

    def _L0_conv_ref(x, gn_gamma, gn_beta, wq, bq, wk, bk, wv, bv):
        import jax, jax.numpy as jnp
        import numpy as np
        GROUPS = 16
        EPS = 0.001

        def group_norm(x, gamma, beta):
            B, H, W, C = x.shape
            xg = x.reshape(B, H, W, GROUPS, C // GROUPS)
            mean = jnp.mean(xg, axis=(1, 2, 4), keepdims=True)
            var = jnp.var(xg, axis=(1, 2, 4), keepdims=True)
            xn = (xg - mean) * jax.lax.rsqrt(var + EPS)
            xn = xn.reshape(B, H, W, C)
            return xn * gamma + beta
        B, H, W, C = x.shape
        h = group_norm(x, gn_gamma, gn_beta)
        hf = h.reshape(B, H * W, C)
        q = hf @ wq + bq
        k = hf @ wk + bk
        v = hf @ wv + bv
        scale = jnp.float32(C) ** (-0.5)
        attn = jnp.einsum('bnc,bmc->bnm', q, k) * scale
        attn = jax.nn.softmax(attn, axis=-1)
        out = jnp.einsum('bnm,bmc->bnc', attn, v)
        return h + out.reshape(B, H, W, C)

    def _L1_conv_ref(x, Wq, bq, Wk, bk, Wv, bv, gamma):
        import jax, jax.numpy as jnp
        import numpy as np
        B, H, W, C = (32, 16, 16, 128)
        C8 = C // 8
        q = jax.nn.relu(jnp.einsum('bhwc,cd->bhwd', x, Wq) + bq)
        k = jax.nn.relu(jnp.einsum('bhwc,cd->bhwd', x, Wk) + bk)
        v = jnp.einsum('bhwc,cd->bhwd', x, Wv) + bv
        scores = jnp.einsum('bhwd,bhvd->bhwv', q, k)
        attn = jax.nn.softmax(scores, axis=-1)
        out = jnp.einsum('bhwv,bhvc->bhwc', attn, v)
        return gamma * out + x

    def _L2_conv_ref(x, Wb, Wc, Wd, gamma):
        import jax, jax.numpy as jnp
        import numpy as np
        H, W = (21, 28)
        B, h, w, C = x.shape
        hw = h * w
        q = jnp.einsum('bhwc,ck->bhwk', x, Wb).reshape(B, hw, C // 8)
        k = jnp.einsum('bhwc,ck->bhwk', x, Wc).reshape(B, hw, C // 8)
        v = jnp.einsum('bhwc,cd->bhwd', x, Wd).reshape(B, hw, C)
        scores = jnp.einsum('bnk,bmk->bnm', q, k)
        attn = jax.nn.softmax(scores, axis=-1)
        ctx = jnp.einsum('bnm,bmd->bnd', attn, v)
        ctx = ctx.reshape(B, h, w, C)
        return gamma * ctx + x

    def _L3_conv_ref(x, w_q, b_q, w_k, b_k, w_v, b_v, w_o, b_o):
        import jax, jax.numpy as jnp
        import numpy as np
        from jax import lax
        N_HEADS = 8
        D_K = 16
        D_V = 16
        TEMP = float(np.sqrt(D_K))

        def avg_pool_3x3_s2_same(x):
            sums = lax.reduce_window(x, 0.0, lax.add, (1, 3, 3, 1), (1, 2, 2, 1), 'SAME')
            ones = jnp.ones(x.shape[:3] + (1,), x.dtype)
            cnt = lax.reduce_window(ones, 0.0, lax.add, (1, 3, 3, 1), (1, 2, 2, 1), 'SAME')
            return sums / cnt

        def conv1x1(x, w, b):
            return jnp.einsum('bhwc,cd->bhwd', x, w) + b
        BS, H, W, C = x.shape
        residual = x
        qt = conv1x1(x, w_q, b_q).reshape(BS * N_HEADS, H * W, -1)
        xp = avg_pool_3x3_s2_same(x)
        kt = conv1x1(xp, w_k, b_k).reshape(BS * N_HEADS, H * W // 4, -1)
        vt = conv1x1(xp, w_v, b_v).reshape(BS * N_HEADS, H * W // 4, -1)
        attn = jnp.einsum('bnd,bmd->bnm', qt, kt) / TEMP
        attn = jax.nn.softmax(attn, axis=-1)
        out = jnp.einsum('bnm,bmd->bnd', attn, vt)
        out = out.reshape(BS, H, W, -1)
        out = conv1x1(out, w_o, b_o)
        return out + residual

    def _gn(v, G=32, eps=1e-05):
        B_, H_, W_, C_ = v.shape
        g = v.reshape(B_, H_, W_, G, C_ // G)
        m = jnp.mean(g, axis=(1, 2, 4), keepdims=True)
        s = jnp.var(g, axis=(1, 2, 4), keepdims=True)
        return ((g - m) / jnp.sqrt(s + eps)).reshape(v.shape)

    def _ln_c(v, eps=1e-06):
        m = jnp.mean(v, axis=-1, keepdims=True)
        s = jnp.var(v, axis=-1, keepdims=True)
        return (v - m) / jnp.sqrt(s + eps)

    def _ln_t(v, eps=1e-05):
        m = jnp.mean(v, axis=-1, keepdims=True)
        s = jnp.var(v, axis=-1, keepdims=True)
        return (v - m) / jnp.sqrt(s + eps)

    def _to_tokens(v):
        B_, H_, W_, C_ = v.shape
        return v.reshape(B_, H_ * W_, C_)

    def _from_tokens(t, like):
        return t.reshape(like.shape)
    x = _L0_conv_ref(x, L0_conv_gn_gamma, L0_conv_gn_beta, L0_conv_wq, L0_conv_bq, L0_conv_wk, L0_conv_bk, L0_conv_wv, L0_conv_bv)
    x = _L1_conv_ref(x, L1_conv_Wq, L1_conv_bq, L1_conv_Wk, L1_conv_bk, L1_conv_Wv, L1_conv_bv, L1_conv_gamma)
    x = _L2_conv_ref(x, L2_conv_Wb, L2_conv_Wc, L2_conv_Wd, L2_conv_gamma)
    x = _L3_conv_ref(x, L3_conv_w_q, L3_conv_b_q, L3_conv_w_k, L3_conv_b_k, L3_conv_w_v, L3_conv_b_v, L3_conv_w_o, L3_conv_b_o)
    return x

_drawn_inputs = setup_inputs


def setup_inputs(seed=0):
    import zlib

    import numpy as np

    out = dict(_drawn_inputs(seed))
    spreads = {'L0_conv_gn_gamma': (1.0, 0.2),
     'L0_conv_gn_beta': (0.0, 0.1),
     'L0_conv_bq': (0.0, 0.8),
     'L0_conv_bk': (0.0, 0.8),
     'L0_conv_bv': (0.0, 0.1),
     'L1_conv_bq': (0.0, 0.333),
     'L1_conv_bk': (0.0, 0.475),
     'L1_conv_bv': (0.0, 0.1),
     'L3_conv_b_q': (0.0, 0.8),
     'L3_conv_b_k': (0.0, 0.8),
     'L3_conv_b_v': (0.0, 0.8),
     'L3_conv_b_o': (0.0, 0.1)}
    factors = {}
    for name, (base, spread) in spreads.items():
        noise = np.random.default_rng([zlib.crc32(name.encode()), seed]).standard_normal(out[name].shape)
        drawn = base * np.exp(spread * noise) if base else spread * noise
        out[name] = jnp.asarray(drawn.astype(out[name].dtype))
    for name, factor in factors.items():
        out[name] = (out[name] * factor).astype(out[name].dtype)
    return out
```

```python
import numpy as np
import concourse.bass as bass
from concourse import mybir
from contextlib import ExitStack

IMAGES, SIDE, C = 8, 16, 128
TOK = SIDE * SIDE
TILES = TOK // 128
SLOTS = 4
ROUNDS = IMAGES // SLOTS
GROUPS = 16
GN_EPS = 1e-3
DQK = C // 8
HEADS, DH = 8, 16
PSIDE = SIDE // 2
PTOK = PSIDE * PSIDE
HKEY = PTOK // HEADS
KEYS = HKEY * HEADS
STRIPS, STRIP = 4, 32
HALVES = HEADS // STRIPS
HTOK = TOK // HEADS
PAIRS = HEADS // 2
BANKS = 8
BLK_ROWS = 128 // SIDE
BIG = float(2 ** 100)
PARTS = 3


def constants():
    ident = np.eye(128, dtype=np.float32)
    group = np.kron(np.eye(GROUPS), np.full((C // GROUPS,) * 2, GROUPS / C)).astype(np.float32)
    n = np.full(PSIDE, 3.0)
    n[-1] = 2.0
    inv_count = np.broadcast_to((1.0 / np.outer(n, n)).reshape(1, PTOK), (128, PTOK)).astype(np.float32)
    pick_v = np.zeros((128, DH), np.float32)
    pick_v[DH:2 * DH] = np.eye(DH)
    f = np.concatenate([ident, group, inv_count, pick_v], axis=1)
    left = np.zeros((128, 128), np.float32)
    right = np.zeros((128, 128), np.float32)
    rows = np.kron(np.eye(BLK_ROWS), np.ones((1, SIDE)))
    left[:BLK_ROWS], left[BLK_ROWS] = rows, 1.0
    right[:BLK_ROWS], right[BLK_ROWS] = rows * BIG, -BIG
    chunk = np.zeros((128, HEADS * PTOK), np.float32)
    for part in range(PARTS):
        chunk[STRIP * part:STRIP * part + HEADS] = np.tile(
            np.kron(np.eye(HEADS), np.ones((1, HKEY))), (1, HEADS))
    return np.ascontiguousarray(f), np.concatenate([left, right, chunk], axis=1)


def build(nc, x, gn_gamma, gn_beta, wq0, bq0, wk0, bk0, wv0, bv0, wq1, bq1, wk1, bk1, wv1, bv1, gamma1,
          wb2, wc2, wd2, gamma2, wq3, bq3, wk3, bk3, wv3, bv3, wo3, bo3, const_f, const_b, out):
    f32, bf16 = mybir.dt.float32, mybir.dt.bfloat16
    ALU, ACT, AX = mybir.AluOpType, mybir.ActivationFunctionType, mybir.AxisListType
    x_v = x.rearrange("b (t a) w c -> b (a w) t c", t=TILES)
    out_v = out.rearrange("b (t a) w c -> b (a w) t c", t=TILES)

    ctx = ExitStack()
    with ctx:
        def sb(name, shape, dt=f32):
            return ctx.enter_context(nc.sbuf_tensor(name, shape, dt))

        def sem(name):
            return ctx.enter_context(nc.semaphore(name))

        consts = sb("consts", [128, 128 + 128 + PTOK + DH])
        ident, group_avg = consts[:, 0:128], consts[:, 128:256]
        inv_count, pick_v = consts[:, 256:256 + PTOK], consts[0:STRIP, 256 + PTOK:256 + PTOK + DH]
        const_bf = sb("const_bf", [128, 256 + HEADS * PTOK], bf16)
        mask_l, mask_r = const_bf[0:BLK_ROWS + 1, 0:128], const_bf[0:BLK_ROWS + 1, 128:256]
        chunk_of = const_bf[0:STRIP * PARTS, 256:256 + HEADS * PTOK]
        w0 = sb("w0", [128, 3, C])
        w1qk, w1v = sb("w1qk", [128, 2, DQK]), sb("w1v", [128, C])
        w2qk, w2v = sb("w2qk", [128, 2, DQK]), sb("w2v", [128, C])
        w3 = sb("w3", [128, 4, C])
        w3q = sb("w3q", [128, HALVES, STRIPS, STRIP])
        w3kv = sb("w3kv", [128, HEADS, STRIPS, 2, DH])
        rows = sb("rows", [16, 128])
        R_GAMMA, R_BETA, R_BQ0, R_BK0, R_BV0, R_BV1, R_BQ1, R_BK1, R_BQ3 = range(9)
        cols = sb("cols", [128, 16])
        gates = sb("gates", [128, 2])
        bo_all = sb("bo_all", [128, 1, C])
        kvb = sb("kvb", [STRIP * PARTS, STRIPS, 2, DH])
        kvb_parts = sb("kvb_parts", [STRIP * PARTS, 128], bf16)

        x_in = [sb(f"x_in{g}", [128, TILES, C]) for g in range(SLOTS)]
        xT = [sb(f"xT{g}", [128, TOK]) for g in range(SLOTS)]
        qT = [sb(f"qT{g}", [128, 2, TOK]) for g in range(SLOTS)]
        v = [sb(f"v{g}", [128, TILES, C]) for g in range(SLOTS)]
        prob = [sb(f"prob{g}", [128, TILES, 512]) for g in range(SLOTS)]
        probT = [sb(f"probT{g}", [128, TILES, 512]) for g in range(SLOTS)]
        negmax = [sb(f"negmax{g}", [128, TILES, HEADS]) for g in range(SLOTS)]
        total = [sb(f"total{g}", [128, TILES]) for g in range(SLOTS)]
        inv = [sb(f"inv{g}", [128, TILES, HEADS]) for g in range(SLOTS)]
        stats = sb("stats", [128, SLOTS, 2, 3])
        means = sb("means", [128, SLOTS])
        spread = sb("spread", [128, SLOTS, 2])
        scale_gn, shift_gn = sb("scale_gn", [128, SLOTS]), sb("shift_gn", [128, SLOTS])
        var_gn, neg_half = sb("var_gn", [128, SLOTS]), sb("neg_half", [128, SLOTS])
        poolW = [sb(f"poolW{g}", [128, SIDE, PSIDE]) for g in range(SLOTS)]
        poolT = [sb(f"poolT{g}", [128, PSIDE, PSIDE]) for g in range(SLOTS)]
        kdiag = [sb(f"kdiag{g}", [128, STRIPS, HEADS * PTOK]) for g in range(SLOTS)]
        vdiag = [sb(f"vdiag{g}", [128, HEADS, 2, DH + 1]) for g in range(SLOTS)]
        o_tok = [sb(f"o_tok{g}", [128, TILES, HEADS, DH]) for g in range(SLOTS)]
        oT = [sb(f"oT{g}", [128, TOK]) for g in range(SLOTS)]
        y_all = sb("y_all", [128, IMAGES, TILES, C])
        bank = [ctx.enter_context(nc.psum_tensor(f"bank{b}", [128, 512], f32)) for b in range(BANKS)]

        order = [("xT", 0, g) for g in range(SLOTS)] + [("group mean", 0, 0), ("group var", 0, 0)]
        for layer in range(3):
            for kind in ("qk", "v", "scores", "probT", "o"):
                order += [(kind, layer, g) for g in range(SLOTS)]
        for kinds in (("kv", "q"), ("vd",), ("scores0", "scores1"), ("probT0", "probT1"), ("pv",), ("oT",), ("y",)):
            order += [(kind, 3, g) for g in range(SLOTS) for kind in kinds]
        place = {tile: n for n, tile in enumerate(order)}
        uses = [len(range(b, len(order), BANKS)) for b in range(BANKS)]

        filled = [sem(f"filled{b}") for b in range(BANKS)]
        drained = [sem(f"drained{b}") for b in range(BANKS)]

        def psum(kind, layer, g=0):
            return bank[place[kind, layer, g] % BANKS]

        def filled_by(kind, layer, g=0):
            return filled[place[kind, layer, g] % BANKS], 1

        def drained_by(kind, layer, g=0):
            return drained[place[kind, layer, g] % BANKS], 1

        def count(rnd, kind, layer, g=0):
            n = place[kind, layer, g]
            return rnd * uses[n % BANKS] + n // BANKS + 1

        def wait_filled(eng, rnd, kind, layer, g=0):
            eng.wait_ge(filled[place[kind, layer, g] % BANKS], count(rnd, kind, layer, g))

        def wait_drained(eng, rnd, kind, layer, g=0):
            eng.wait_ge(drained[place[kind, layer, g] % BANKS], count(rnd, kind, layer, g) + 1)

        def view(ap, n):
            return ap.rearrange("p (n f) -> p n f", n=n)

        s_consts, s_w0, s_w1, s_w3, s_rows, s_kvb, s_bo, s_gate = (sem(n) for n in (
            "consts_loaded", "w0_loaded", "w12_loaded", "w3_loaded", "rows_loaded", "kvb_loaded", "bo_loaded", "gates_loaded"))
        s_x = [sem(f"x_loaded{g}") for g in range(SLOTS)]
        s_y = sem("y_stored")
        s_zero, s_ones, s_arranged, s_kvb_part = sem("zeros_set"), sem("ones_set"), sem("weights_arranged"), sem("kv_bias_step")
        s_cols_ps, s_cols, s_gated = sem("bias_rows_turned"), sem("bias_columns_ready"), sem("gates_applied")
        s_norm, s_moments = sem("norm_step"), sem("channel_moments")
        s_max, s_inv, s_scaled = sem("max_ready"), sem("inv_ready"), sem("prob_scaled")
        s_pool, s_rstd = sem("pool_step"), sem("inverse_deviations")
        s_strips, s_max3, s_exp3, s_inv3 = sem("kdiag_strips"), sem("max3_ready"), sem("exp3_ready"), sem("inv3_ready")

        def unit(rnd, layer, g):
            return rnd * 3 * SLOTS + layer * SLOTS + g + 1

        def image(rnd, g, each=1, k=0):
            return rnd * SLOTS * each + g * each + k + 1

        POOL_STEPS = 5
        KVB_STEPS = 1 + PARTS * (PARTS - 1)
        NORM_STEPS = 6
        bias = [cols[:, r:r + 1] for r in range(16)]
        block = ctx.enter_context(nc.Block())

        @block.sync
        def _(sp):
            sp.dma_start(x_in[0][:, :, :], x_v[0]).then_inc(s_x[0], 16)
            sp.dma_start(consts[:, :], const_f).then_inc(s_consts, 16)
            for g in range(1, SLOTS):
                sp.dma_start(x_in[g][:, :, :], x_v[g]).then_inc(s_x[g], 16)
            for n, w in enumerate((wq0, wk0, wv0)):
                sp.dma_start(w0[:, n, :], w).then_inc(s_w0, 16)
            for n, w in enumerate((wq3, wk3, wv3, wo3)):
                sp.dma_start(w3[:, n, :], w).then_inc(s_w3, 16)
            for rnd in range(ROUNDS):
                if rnd + 1 < ROUNDS:
                    for g in range(SLOTS):
                        wait_filled(sp, rnd, "xT", 0, g)
                        sp.dma_start(x_in[g][:, :, :], x_v[(rnd + 1) * SLOTS + g]).then_inc(s_x[g], 16)
                for g in range(SLOTS):
                    wait_drained(sp, rnd, "y", 3, g)
                    sp.dma_start(out_v[rnd * SLOTS + g], y_all[:, rnd * SLOTS + g, :, :]).then_inc(s_y, 16)
            sp.wait_ge(s_y, 16 * IMAGES)

        @block.gpsimd
        def _(pool):
            nc.gpsimd.memset(rows[:, :], 0.0).then_inc(s_zero, 1)
            nc.gpsimd.memset(neg_half[:, :], -0.5).then_inc(s_zero, 1)
            nc.gpsimd.memset(w3q[:, :, :, :], 0.0).then_inc(s_zero, 1)
            nc.gpsimd.memset(kvb[:, :, :, :], 0.0).then_inc(s_zero, 1)
            for g in range(SLOTS):
                nc.gpsimd.memset(vdiag[g][:, :, :, :], 0.0).then_inc(s_zero, 1)
            for g in range(SLOTS):
                nc.gpsimd.memset(kdiag[g][:, :, :], 0.0).then_inc(s_zero, 1)
            pool.wait_ge(s_w1, 16 * 6)
            pool.wait_ge(s_gate, 16 * 2)
            nc.gpsimd.tensor_scalar(w1v[:, :], w1v[:, :], gates[:, 0:1], None, ALU.mult).then_inc(s_gated, 1)
            nc.gpsimd.tensor_scalar(w2v[:, :], w2v[:, :], gates[:, 1:2], None, ALU.mult).then_inc(s_gated, 1)
            pool.wait_ge(s_zero, 4)
            pool.wait_ge(s_w3, 16 * 4)
            for a in range(HALVES):
                src = w3[:, 0, 64 * a:64 * a + 64].rearrange("p (b d) -> p b d", d=DH)
                nc.gpsimd.tensor_copy(w3q[:, a, :, 0:DH], src).then_inc(s_arranged, 1)
            for kind in range(2):
                for b in range(STRIPS):
                    src = w3[:, 1 + kind, :].rearrange("p (c d) -> p c d", d=DH)
                    nc.gpsimd.tensor_copy(w3kv[:, :, b, kind, :], src).then_inc(s_arranged, 1)
            with pool.Fori(0, ROUNDS) as rnd:
                wait_drained(pool, rnd, "group var", 0)
                nc.gpsimd.tensor_tensor(var_gn[:, :], var_gn[:, :], neg_half[:, :], ALU.pow).then_inc(s_rstd, 1)
                for layer in range(3):
                    for g in range(SLOTS):
                        pool.wait_ge(s_inv, unit(rnd, layer, g))
                        for t in range(TILES):
                            keys = 128 if layer == 1 else TOK
                            last = nc.gpsimd.tensor_tensor(prob[g][:, t, 0:keys], prob[g][:, t, 0:keys],
                                                           inv[g][:, t, 0:1].broadcast_to([128, keys]), ALU.mult)
                        last.then_inc(s_scaled, 1)
                for g in range(SLOTS):
                    wait_drained(pool, rnd, "o", 2, g)
                    xi = xT[g][:, :].rearrange("p (h w) -> p h w", w=SIDE)
                    w, p = poolW[g], poolT[g]
                    steps = iter(range(POOL_STEPS))

                    def add(out, in0, in1, op=ALU.add):
                        k = next(steps)
                        if k:
                            pool.wait_ge(s_pool, image(rnd, g, POOL_STEPS, k - 1))
                        nc.gpsimd.tensor_tensor(out, in0, in1, op).then_inc(s_pool, 1)
                    add(w[:, :, :], xi[:, :, 0::2], xi[:, :, 1::2])
                    add(w[:, :, 0:PSIDE - 1], w[:, :, 0:PSIDE - 1], xi[:, :, 2::2])
                    add(p[:, :, :], w[:, 0::2, :], w[:, 1::2, :])
                    add(p[:, 0:PSIDE - 1, :], p[:, 0:PSIDE - 1, :], w[:, 2::2, :])
                    add(p[:, :, :], p[:, :, :], inv_count.rearrange("p (h w) -> p h w", w=PSIDE), ALU.mult)

        @block.scalar
        def _(act):
            for n, w in enumerate((wq1, wk1)):
                act.dma_start(w1qk[:, n, :], w).then_inc(s_w1, 16)
            for n, w in enumerate((wb2, wc2)):
                act.dma_start(w2qk[:, n, :], w).then_inc(s_w1, 16)
            act.dma_start(w1v[:, :], wv1).then_inc(s_w1, 16)
            act.dma_start(w2v[:, :], wd2).then_inc(s_w1, 16)
            for n, gate in enumerate((gamma1, gamma2)):
                act.dma_start(gates[:, n:n + 1], gate.rearrange("(a n) -> a n", a=1).partition_broadcast(128)).then_inc(s_gate, 16)
            act.wait_ge(s_zero, 4)
            for r, b in ((R_GAMMA, gn_gamma), (R_BETA, gn_beta), (R_BQ0, bq0), (R_BK0, bk0), (R_BV0, bv0),
                         (R_BV1, bv1), (R_BQ1, bq1), (R_BK1, bk1)):
                act.dma_start(rows[r:r + 1, 0:b.shape[0]], b.rearrange("(a n) -> a n", a=1)).then_inc(s_rows, 16)
            act.dma_start(rows[R_BQ3:R_BQ3 + 2, :].rearrange("a (b e) -> a b e", e=STRIP)[:, :, 0:DH],
                          bq3.rearrange("(a b d) -> a b d", b=STRIPS, d=DH)).then_inc(s_rows, 16)
            for part in range(PARTS):
                for kind, b in ((0, bk3), (1, bv3)):
                    for strip in range(STRIPS):
                        act.dma_start(kvb[STRIP * part:STRIP * part + HEADS, strip, kind, :],
                                      b.rearrange("(c d) -> c d", d=DH)).then_inc(s_kvb, 16)
            act.dma_start(bo_all[:, 0, :], bo3.rearrange("(a n) -> a n", a=1).partition_broadcast(128)).then_inc(s_bo, 16)
            act.dma_start(const_bf[:, :], const_b).then_inc(s_consts, 16)
            with act.Fori(0, ROUNDS) as rnd:
                for layer in range(3):
                    if layer == 2:
                        for g in range(SLOTS):
                            wait_filled(act, rnd, "qk", layer, g)
                            nc.scalar.activation(qT[g][0:DQK, :, :], view(psum("qk", layer, g)[0:DQK, :], 2), ACT.Copy)\
                                .then_inc(*drained_by("qk", layer, g))
                    for g in range(SLOTS):
                        wait_filled(act, rnd, "v", layer, g)
                        nc.scalar.activation(v[g][:, :, :], view(psum("v", layer, g)[:, 0:TOK], TILES), ACT.Copy)\
                            .then_inc(*drained_by("v", layer, g))
                    keys = 128 if layer == 1 else TOK
                    for g in range(SLOTS):
                        act.wait_ge(s_max, unit(rnd, layer, g))
                        for t in range(TILES):
                            last = nc.scalar.activation(prob[g][:, t, 0:keys], psum("scores", layer, g)[:, keys * t:keys * t + keys],
                                                        ACT.Exp, bias=negmax[g][:, t, 0:1], accum_out=total[g][:, t:t + 1])
                        last.then_inc(*drained_by("scores", layer, g))
                    for g in range(SLOTS):
                        wait_filled(act, rnd, "probT", layer, g)
                        nc.scalar.activation(probT[g][:, 0, 0:TILES * keys], psum("probT", layer, g)[:, 0:TILES * keys], ACT.Copy)\
                            .then_inc(*drained_by("probT", layer, g))
                for g in range(SLOTS):
                    wait_filled(act, rnd, "kv", 3, g)
                    act.wait_ge(s_zero, 4 + 2 * SLOTS)
                    for b in range(2, STRIPS):
                        part = slice(STRIP * b, STRIP * b + STRIP)
                        if b == STRIPS - 1:
                            act.wait_ge(s_strips, image(rnd, g))
                        last = nc.scalar.activation(kdiag[g][part, b, :], psum("kv", 3, g)[part, :], ACT.Copy)
                    last.then_inc(*drained_by("kv", 3, g))
                for g in range(SLOTS):
                    wait_filled(act, rnd, "vd", 3, g)
                    for c2 in range(2):
                        part = slice(KEYS * c2, KEYS * c2 + KEYS)
                        last = nc.scalar.activation(vdiag[g][part, :, c2, 0:DH],
                                                    view(psum("vd", 3, g)[part, 0:C], HEADS), ACT.Copy)
                    last.then_inc(*drained_by("vd", 3, g))
                for g in range(SLOTS):
                    for t in range(TILES):
                        wait_drained(act, rnd, f"scores{t}", 3, g)
                        nc.scalar.activation(prob[g][:, t, :], prob[g][:, t, :], ACT.Exp).then_inc(s_exp3, 1)
                for g in range(SLOTS):
                    for t in range(TILES):
                        wait_filled(act, rnd, f"probT{t}", 3, g)
                        nc.scalar.activation(probT[g][:, t, :], psum(f"probT{t}", 3, g)[:, :], ACT.Copy)\
                            .then_inc(*drained_by(f"probT{t}", 3, g))
                for g in range(SLOTS):
                    wait_filled(act, rnd, "oT", 3, g)
                    nc.scalar.activation(oT[g][:, :], psum("oT", 3, g)[:, 0:TOK], ACT.Copy).then_inc(*drained_by("oT", 3, g))

        @block.vector
        def _(dve):
            flat = kvb[:, :, :, :].rearrange("p b k d -> p (b k d)")
            dve.wait_ge(s_kvb, 16 * PARTS * 2 * STRIPS)
            nc.vector.tensor_copy(kvb_parts[:, :], flat).then_inc(s_kvb_part, 1)
            steps = 1
            for part in range(1, PARTS):
                for at in (slice(STRIP * p, STRIP * p + STRIP) for p in range(part, PARTS)):
                    dve.wait_ge(s_kvb_part, steps)
                    nc.vector.tensor_tensor(flat[at], flat[at], kvb_parts[at, :], ALU.subtract).then_inc(s_kvb_part, 1)
                    dve.wait_ge(s_kvb_part, steps + 1)
                    nc.vector.tensor_copy(kvb_parts[at, :], flat[at]).then_inc(s_kvb_part, 1)
                    steps += 2
            assert steps == KVB_STEPS
            dve.wait_ge(s_zero, 4 + SLOTS)
            for g in range(SLOTS):
                for c2 in range(2):
                    nc.vector.memset(vdiag[g][KEYS * c2:KEYS * c2 + KEYS, :, c2, DH:DH + 1], 1.0).then_inc(s_ones, 1)
            dve.wait_ge(s_cols_ps, 1)
            nc.vector.tensor_copy(cols[:, :], bank[BANKS - 1][:, 0:16]).then_inc(s_cols, 1)
            dve.wait_ge(s_cols, 1)
            dve.wait_ge(s_gate, 16 * 2)
            nc.vector.tensor_scalar(cols[:, R_BV1:R_BV1 + 1], bias[R_BV1], gates[:, 0:1], None, ALU.mult).then_inc(s_cols, 1)
            dve.wait_ge(s_cols, 2)
            with dve.Fori(0, ROUNDS) as rnd:
                done = [0]

                def link(ins):
                    ins.then_inc(s_norm, 1)
                    done[0] += 1
                    dve.wait_ge(s_norm, rnd * NORM_STEPS + done[0])

                for g in range(SLOTS):
                    wait_filled(dve, rnd, "xT", 0, g)
                    nc.vector.bn_stats(stats[:, g, :, :], psum("xT", 0, g)[:, 0:TOK]).then_inc(s_moments, 1)
                wait_filled(dve, rnd, "group mean", 0)
                link(nc.vector.tensor_scalar(means[:, :], psum("group mean", 0)[:, 0:SLOTS], 0.5, None, ALU.mult))
                link(nc.vector.tensor_tensor(spread[:, :, :], stats[:, :, :, 1],
                                             means[:, :].unsqueeze(2).broadcast_to([128, SLOTS, 2]), ALU.subtract))
                link(nc.vector.tensor_tensor(spread[:, :, :], spread[:, :, :], spread[:, :, :], ALU.mult))
                nc.vector.scalar_tensor_tensor(out=spread[:, :, :], in0=stats[:, :, :, 2], scalar=2.0 / TOK, in1=spread[:, :, :],
                                               op0=ALU.mult, op1=ALU.add).then_inc(*drained_by("group mean", 0))
                wait_filled(dve, rnd, "group var", 0)
                nc.vector.tensor_scalar(var_gn[:, :], psum("group var", 0)[:, 0:SLOTS], 0.5, GN_EPS, ALU.mult, ALU.add)\
                    .then_inc(*drained_by("group var", 0))
                dve.wait_ge(s_rstd, rnd + 1)
                link(nc.vector.tensor_scalar(scale_gn[:, :], var_gn[:, :], bias[R_GAMMA], None, ALU.mult))
                link(nc.vector.tensor_tensor(means[:, :], means[:, :], scale_gn[:, :], ALU.mult))
                link(nc.vector.tensor_scalar(shift_gn[:, :], means[:, :], -1.0, bias[R_BETA], ALU.mult, ALU.add))
                assert done[0] == NORM_STEPS
                for g in range(SLOTS):
                    nc.vector.tensor_scalar(xT[g][:, :], psum("xT", 0, g)[:, 0:TOK], scale_gn[:, g:g + 1],
                                            shift_gn[:, g:g + 1], ALU.mult, ALU.add).then_inc(*drained_by("xT", 0, g))
                for layer in range(3):
                    if layer < 2:
                        for g in range(SLOTS):
                            wait_filled(dve, rnd, "qk", layer, g)
                            ps = psum("qk", layer, g)
                            if layer == 0:
                                nc.vector.tensor_scalar(qT[g][:, 0, :], ps[:, 0:TOK], bias[R_BQ0], float(C) ** -0.5, ALU.add, ALU.mult)
                                nc.vector.tensor_scalar(qT[g][:, 1, :], ps[:, TOK:], bias[R_BK0], None, ALU.add)\
                                    .then_inc(*drained_by("qk", layer, g))
                            else:
                                nc.vector.tensor_scalar(qT[g][0:DQK, 0, :], ps[0:DQK, 0:TOK], bias[R_BQ1][0:DQK], 0.0, ALU.add, ALU.max)
                                nc.vector.tensor_scalar(qT[g][0:DQK, 1, :], ps[0:DQK, TOK:], bias[R_BK1][0:DQK], 0.0, ALU.add, ALU.max)\
                                    .then_inc(*drained_by("qk", layer, g))
                    keys = 128 if layer == 1 else TOK
                    for g in range(SLOTS):
                        wait_filled(dve, rnd, "scores", layer, g)
                        nc.vector.tensor_reduce(out=negmax[g][:, :, 0], in_=view(psum("scores", layer, g)[:, 0:TILES * keys], TILES),
                                                op=ALU.max, axis=AX.X, negate=True).then_inc(s_max, 1)
                    for g in range(SLOTS):
                        wait_drained(dve, rnd, "scores", layer, g)
                        nc.vector.reciprocal(inv[g][:, :, 0], total[g][:, :]).then_inc(s_inv, 1)
                    for g in range(SLOTS):
                        wait_filled(dve, rnd, "o", layer, g)
                        ps = psum("o", layer, g)[:, 0:TOK]
                        if layer < 2:
                            last = nc.vector.scalar_tensor_tensor(out=xT[g][:, :], in0=ps, scalar=bias[(R_BV0, R_BV1)[layer]],
                                                                  in1=xT[g][:, :], op0=ALU.add, op1=ALU.add)
                        else:
                            last = nc.vector.tensor_tensor(xT[g][:, :], ps, xT[g][:, :], ALU.add)
                        last.then_inc(*drained_by("o", layer, g))
                for g in range(SLOTS):
                    wait_filled(dve, rnd, "kv", 3, g)
                    if g == 0:
                        dve.wait_ge(s_zero, 4 + 2 * SLOTS)
                    for b in range(2):
                        part = slice(STRIP * b, STRIP * b + STRIP)
                        last = nc.vector.tensor_copy(kdiag[g][part, b, :], psum("kv", 3, g)[part, :])
                    last.then_inc(s_strips, 1)
                    wait_filled(dve, rnd, "q", 3, g)
                    for a in range(HALVES):
                        last = nc.vector.tensor_scalar(qT[g][:, a, :], psum("q", 3, g)[:, TOK * a:TOK * a + TOK],
                                                       bias[R_BQ3 + a], float(DH) ** -0.5, ALU.add, ALU.mult)
                    last.then_inc(*drained_by("q", 3, g))
                for g in range(SLOTS):
                    for t in range(TILES):
                        wait_filled(dve, rnd, f"scores{t}", 3, g)
                        s3 = view(psum(f"scores{t}", 3, g)[:, :], HEADS)
                        nc.vector.tensor_reduce(out=negmax[g][:, t, :], in_=s3, op=ALU.max, axis=AX.X, negate=True).then_inc(s_max3, 1)
                        dve.wait_ge(s_max3, image(rnd, g, TILES, t))
                        nc.vector.tensor_tensor(view(prob[g][:, t, :], HEADS), s3,
                                                negmax[g][:, t, :].unsqueeze(2).broadcast_to([128, HEADS, KEYS]), ALU.add)\
                            .then_inc(*drained_by(f"scores{t}", 3, g))
                for g in range(SLOTS):
                    wait_filled(dve, rnd, "pv", 3, g)
                    pv = psum("pv", 3, g)[:, 0:TILES * HEADS * (DH + 1)].rearrange("p (c e) -> p c e", e=DH + 1)
                    inv3 = inv[g][:, :, :].rearrange("p t c -> p (t c)")
                    nc.vector.reciprocal(inv3, pv[:, :, DH]).then_inc(s_inv3, 1)
                    dve.wait_ge(s_inv3, image(rnd, g))
                    nc.vector.tensor_tensor(o_tok[g][:, :, :, :].rearrange("p t c d -> p (t c) d"), pv[:, :, 0:DH],
                                            inv3.unsqueeze(2).broadcast_to([128, TILES * HEADS, DH]), ALU.mult)\
                        .then_inc(*drained_by("pv", 3, g))
                for g in range(SLOTS):
                    wait_filled(dve, rnd, "y", 3, g)
                    if g == 0:
                        dve.wait_ge(s_bo, 16)
                    nc.vector.tensor_tensor(y_all[:, bass.ds(rnd * SLOTS + g, 1), :, :].rearrange(
                        "p o t c -> p (o t) c"), view(psum("y", 3, g)[:, 0:TOK], TILES),
                                            bo_all[:, :, :].broadcast_to([128, TILES, C]), ALU.add).then_inc(*drained_by("y", 3, g))

        @block.tensor
        def _(pe):
            mm = nc.tensor.matmul
            for b in range(BANKS):
                pe.sem_inc(drained[b], 1)
            pe.wait_ge(s_consts, 16 * 2)
            pe.wait_ge(s_rows, 16 * 9)
            nc.tensor.transpose(bank[BANKS - 1][:, 0:16], rows[:, :], ident[0:16, 0:16]).then_inc(s_cols_ps, 1)
            with pe.Fori(0, ROUNDS) as rnd:
                def begin(kind, layer, g=0):
                    pe.wait_ge(drained[place[kind, layer, g] % BANKS], count(rnd, kind, layer, g))
                    return psum(kind, layer, g)

                for g in range(SLOTS):
                    pe.wait_ge(s_x[g], 16 * rnd + 16)
                    ps = begin("xT", 0, g)
                    for t in range(TILES):
                        last = nc.tensor.transpose(ps[:, 128 * t:128 * t + 128], x_in[g][:, t, :], ident)
                    last.then_inc(*filled_by("xT", 0, g))
                pe.wait_ge(s_moments, SLOTS * rnd + SLOTS)
                ps = begin("group mean", 0)
                for half in range(2):
                    last = mm(ps[:, 0:SLOTS], group_avg, stats[:, :, half, 1], start=half == 0, stop=half == 1)
                last.then_inc(*filled_by("group mean", 0))
                wait_drained(pe, rnd, "group mean", 0)
                ps = begin("group var", 0)
                for half in range(2):
                    last = mm(ps[:, 0:SLOTS], group_avg, spread[:, :, half], start=half == 0, stop=half == 1)
                last.then_inc(*filled_by("group var", 0))
                pe.wait_ge(s_w0, 16 * 3)
                pe.wait_ge(s_w1, 16 * 6)
                pe.wait_ge(s_gated, 2)
                pe.wait_ge(s_cols, 2)
                for layer in range(3):
                    wqk = (w0[:, 0:2, :], w1qk[:, :, :], w2qk[:, :, :])[layer]
                    wv = (w0[:, 2, :], w1v[:, :], w2v[:, :])[layer]
                    width = C if layer == 0 else DQK
                    keys = 128 if layer == 1 else TOK
                    for g in range(SLOTS):
                        if layer == 0:
                            wait_drained(pe, rnd, "xT", 0, g)
                        else:
                            wait_drained(pe, rnd, "o", layer - 1, g)
                        ps = begin("qk", layer, g)
                        for n in range(2):
                            last = mm(ps[0:width, TOK * n:TOK * n + TOK], wqk[:, n, :], xT[g][:, :], start=True, stop=True)
                        last.then_inc(*filled_by("qk", layer, g))
                    for g in range(SLOTS):
                        ps = begin("v", layer, g)
                        for t in range(TILES):
                            last = mm(ps[:, C * t:C * t + C], xT[g][:, 128 * t:128 * t + 128], wv, start=True, stop=True)
                        last.then_inc(*filled_by("v", layer, g))
                    for g in range(SLOTS):
                        wait_drained(pe, rnd, "qk", layer, g)
                        ps = begin("scores", layer, g)
                        for t in range(TILES):
                            q = qT[g][0:width, 0, 128 * t:128 * t + 128]
                            if layer == 1:
                                mm(ps[:, 128 * t:128 * t + 128], q, qT[g][0:width, 1, 128 * t:128 * t + 128], start=True, stop=False)
                                last = mm(ps[:, 128 * t:128 * t + 128], mask_l, mask_r, start=False, stop=True)
                            else:
                                last = mm(ps[:, TOK * t:TOK * t + TOK], q, qT[g][0:width, 1, :], start=True, stop=True)
                        last.then_inc(*filled_by("scores", layer, g))
                    for g in range(SLOTS):
                        pe.wait_ge(s_scaled, unit(rnd, layer, g))
                        ps = begin("probT", layer, g)
                        for k in range(keys // 128):
                            for t in range(TILES):
                                last = nc.tensor.transpose(ps[:, TOK * k + 128 * t:TOK * k + 128 * t + 128],
                                                           prob[g][:, t, 128 * k:128 * k + 128], ident)
                        last.then_inc(*filled_by("probT", layer, g))
                    for g in range(SLOTS):
                        wait_drained(pe, rnd, "v", layer, g)
                        wait_drained(pe, rnd, "probT", layer, g)
                        ps = begin("o", layer, g)
                        if layer == 1:
                            for t in range(TILES):
                                last = mm(ps[:, 128 * t:128 * t + 128], v[g][:, t, :], probT[g][:, 0, 128 * t:128 * t + 128],
                                          start=True, stop=True)
                        else:
                            for k in range(TILES):
                                last = mm(ps[:, 0:TOK], v[g][:, k, :], probT[g][:, 0, TOK * k:TOK * k + TOK],
                                          start=k == 0, stop=k == TILES - 1)
                        last.then_inc(*filled_by("o", layer, g))
                pe.wait_ge(s_arranged, HALVES + 2 * STRIPS)
                pe.wait_ge(s_kvb_part, KVB_STEPS)
                pe.wait_ge(s_ones, 2 * SLOTS)
                for g in range(SLOTS):
                    pe.wait_ge(s_pool, image(rnd, g, POOL_STEPS, POOL_STEPS - 1))
                    ps = begin("kv", 3, g)
                    mm(ps[:, :], kvb_parts[:, :], chunk_of, start=True, stop=False, skip_group_check=True)
                    for c in range(HEADS):
                        last = mm(ps[:, :].rearrange("p (j c m) -> p j c m", j=HEADS, c=HEADS)[:, :, c, :], w3kv[:, c, :, :, :].rearrange("p b k d -> p (b k d)"),
                                  poolT[g][:, :, :], start=False, stop=c == HEADS - 1,
                                  skip_group_check=True)
                    last.then_inc(*filled_by("kv", 3, g))
                    ps = begin("q", 3, g)
                    for a in range(HALVES):
                        for b in range(STRIPS):
                            last = mm(ps[STRIP * b:STRIP * b + STRIP, TOK * a:TOK * a + TOK], w3q[:, a, b, :], xT[g][:, :],
                                      start=True, stop=True)
                    last.then_inc(*filled_by("q", 3, g))
                for g in range(SLOTS):
                    wait_drained(pe, rnd, "kv", 3, g)
                    ps = begin("vd", 3, g)
                    for j in range(HEADS):
                        for c2 in range(2):
                            last = mm(ps[KEYS * c2:KEYS * c2 + KEYS, DH * j:DH * j + DH], kdiag[g][0:STRIP, 0, KEYS * j:KEYS * j + KEYS], pick_v,
                                      start=True, stop=True)
                    last.then_inc(*filled_by("vd", 3, g))
                for g in range(SLOTS):
                    wait_drained(pe, rnd, "q", 3, g)
                    for t in range(TILES):
                        ps = begin(f"scores{t}", 3, g)
                        for a in range(HALVES):
                            for s in range(STRIPS):
                                j = STRIPS * t + s
                                last = mm(ps[STRIP * s:STRIP * s + STRIP, TOK * a:TOK * a + TOK].rearrange(
                                              "p (b m) -> p b m", b=STRIPS),
                                          qT[g][:, a, HTOK * j:HTOK * j + HTOK], kdiag[g][:, :, KEYS * j:KEYS * j + KEYS],
                                          start=True, stop=True)
                        last.then_inc(*filled_by(f"scores{t}", 3, g))
                for g in range(SLOTS):
                    for t in range(TILES):
                        pe.wait_ge(s_exp3, image(rnd, g, TILES, t))
                        ps = begin(f"probT{t}", 3, g)
                        for p in range(PAIRS):
                            last = nc.tensor.transpose(ps[:, 128 * p:128 * p + 128], prob[g][:, t, 128 * p:128 * p + 128], ident)
                        last.then_inc(*filled_by(f"probT{t}", 3, g))
                for g in range(SLOTS):
                    wait_drained(pe, rnd, "vd", 3, g)
                    ps = begin("pv", 3, g)
                    for t in range(TILES):
                        wait_drained(pe, rnd, f"probT{t}", 3, g)
                        for p in range(PAIRS):
                            for s in range(STRIPS):
                                at = (t * PAIRS + p) * 2 * (DH + 1)
                                last = mm(ps[STRIP * s:STRIP * s + STRIP, at:at + 2 * (DH + 1)],
                                          probT[g][:, t, 128 * p + STRIP * s:128 * p + STRIP * s + STRIP],
                                          vdiag[g][:, STRIPS * t + s, :, :].rearrange("p c e -> p (c e)"), start=True, stop=True)
                    last.then_inc(*filled_by("pv", 3, g))
                for g in range(SLOTS):
                    wait_drained(pe, rnd, "pv", 3, g)
                    ps = begin("oT", 3, g)
                    for t in range(TILES):
                        last = nc.tensor.transpose(ps[:, 128 * t:128 * t + 128],
                                                   o_tok[g][:, t, :, :].rearrange("p c d -> p (c d)"), ident)
                    last.then_inc(*filled_by("oT", 3, g))
                for g in range(SLOTS):
                    wait_drained(pe, rnd, "oT", 3, g)
                    ps = begin("y", 3, g)
                    for t in range(TILES):
                        mm(ps[:, C * t:C * t + C], oT[g][:, 128 * t:128 * t + 128], w3[:, 3, :], start=True, stop=False)
                        last = mm(ps[:, C * t:C * t + C], xT[g][:, 128 * t:128 * t + 128], ident, start=False, stop=True)
                    last.then_inc(*filled_by("y", 3, g))


_NAMES = ["x", "L0_conv_gn_gamma", "L0_conv_gn_beta", "L0_conv_wq", "L0_conv_bq", "L0_conv_wk", "L0_conv_bk", "L0_conv_wv",
          "L0_conv_bv", "L1_conv_Wq", "L1_conv_bq", "L1_conv_Wk", "L1_conv_bk", "L1_conv_Wv", "L1_conv_bv", "L1_conv_gamma",
          "L2_conv_Wb", "L2_conv_Wc", "L2_conv_Wd", "L2_conv_gamma", "L3_conv_w_q", "L3_conv_b_q", "L3_conv_w_k", "L3_conv_b_k",
          "L3_conv_w_v", "L3_conv_b_v", "L3_conv_w_o", "L3_conv_b_o"]


def kernel(**inputs):
    import numpy as _np
    import ml_dtypes as _mld
    import concourse.bacc as _bacc
    from concourse import mybir as _mybir
    from concourse.bass_utils import run_bass_kernel_spmd as _run

    nc = _bacc.Bacc("TRN2", target_bir_lowering=False, num_devices=1)
    const_f, const_b = constants()
    given = [(name, _np.ascontiguousarray(inputs[name])) for name in _NAMES]
    given += [("const_f", const_f), ("const_b", const_b.astype(_mld.bfloat16))]
    arrays, args = {}, []
    for name, a in given:
        arrays[f"in_{name}_dram"] = a
        args.append(nc.dram_tensor(f"in_{name}_dram", a.shape, _mybir.dt.from_np(a.dtype), kind="ExternalInput").ap())
    args.append(nc.dram_tensor("out_0_dram", (IMAGES, SIDE, SIDE, C), _mybir.dt.float32, kind="ExternalOutput").ap())
    build(nc, *args)
    r = _run(nc, [arrays], core_ids=[0])
    return r.results[0]["out_0_dram"]
```

```python
import numpy as np
import concourse.bass as bass
from concourse import mybir
from contextlib import ExitStack

IMAGES, SIDE, C = 8, 16, 128
TOK = SIDE * SIDE
TILES = TOK // 128
GROUPS = 16
GN_EPS = 1e-3
DQK = C // 8
HEADS, DH = 8, 16
PSIDE = SIDE // 2
PTOK = PSIDE * PSIDE
HKEY = PTOK // HEADS
KEYS = HKEY * HEADS
STRIPS, STRIP = 4, 32
HALVES = HEADS // STRIPS
HTOK = TOK // HEADS
PAIRS = HEADS // 2
BANKS = 8
BLK_ROWS = 128 // SIDE
NORM_IMAGES = 4
BIG = float(2 ** 100)
PARTS = 3


def constants():
    n = np.full(PSIDE, 3.0)
    n[-1] = 2.0
    pick_v = np.zeros((128, DH))
    pick_v[DH:2 * DH] = np.eye(DH)
    f = {"ident": np.eye(128), "group_avg": np.kron(np.eye(GROUPS), np.full((C // GROUPS,) * 2, GROUPS / C)),
         "inv_count": np.broadcast_to((1.0 / np.outer(n, n)).reshape(1, PTOK), (128, PTOK)), "pick_v": pick_v}
    left, right = np.zeros((128, 128)), np.zeros((128, 128))
    rows = np.kron(np.eye(BLK_ROWS), np.ones((1, SIDE)))
    left[:BLK_ROWS], left[BLK_ROWS] = rows, 1.0
    right[:BLK_ROWS], right[BLK_ROWS] = rows * BIG, -BIG
    chunk = np.zeros((128, HEADS * PTOK))
    for part in range(PARTS):
        chunk[STRIP * part:STRIP * part + HEADS] = np.tile(np.kron(np.eye(HEADS), np.ones((1, HKEY))), (1, HEADS))
    b = {"mask_left": left, "mask_right": right, "chunk_of": chunk}
    return {k: v.astype(np.float32) for k, v in f.items()}, {k: v.astype(np.float32) for k, v in b.items()}


def arrange(i):
    def column(v):
        out = np.zeros((128, 1), np.float32)
        out[:v.shape[0], 0] = v
        return out

    def everywhere(v):
        return np.broadcast_to(v.reshape(1, -1), (128, v.size))

    def strips(w):
        out = np.zeros((w.shape[0], HEADS, STRIP), np.float32)
        out[:, :, 0:DH] = w.reshape(-1, HEADS, DH)
        return out.reshape(w.shape[0], HALVES * 128)

    def pair(k, v):
        both = np.stack([k.reshape(-1, HEADS, DH), v.reshape(-1, HEADS, DH)], axis=2)
        return np.repeat(both[:, :, None], STRIPS, axis=2)

    qk1 = np.zeros((128, 64), np.float32)
    qk1[:, 0:DQK], qk1[:, STRIP:STRIP + DQK] = i["L1_conv_Wq"], i["L1_conv_Wk"]
    turned2 = np.zeros((128, 2 * C), np.float32)
    turned2[:DQK, :C], turned2[:DQK, C:] = i["L2_conv_Wb"].T, i["L2_conv_Wc"].T
    bq3 = strips(i["L3_conv_b_q"].reshape(1, C)).reshape(HALVES, 128)
    bkv3 = np.zeros((128, 128), np.float32)
    for part in range(PARTS):
        bkv3[STRIP * part:STRIP * part + HEADS] = pair(i["L3_conv_b_k"], i["L3_conv_b_v"]).reshape(HEADS, 128)
    return [
        {"w0q": i["L0_conv_wq"], "w0k": i["L0_conv_wk"], "w0v": i["L0_conv_wv"],
         "gn_gamma": column(i["L0_conv_gn_gamma"]), "gn_beta": column(i["L0_conv_gn_beta"]),
         "bq0": column(i["L0_conv_bq"]), "bk0": column(i["L0_conv_bk"]), "bv0": column(i["L0_conv_bv"]),
         "bq1": column(i["L1_conv_bq"]), "bk1": column(i["L1_conv_bk"]), "bv1": column(i["L1_conv_bv"]),
         "gamma1": everywhere(i["L1_conv_gamma"]), "gamma2": everywhere(i["L2_conv_gamma"]), "bq3": bq3.T},
        {"w1qk": qk1, "w1v": i["L1_conv_Wv"], "w2qk_turned": turned2, "w2v": i["L2_conv_Wd"]},
        {"w3q": strips(i["L3_conv_w_q"]), "w3o": i["L3_conv_w_o"], "bo3": everywhere(i["L3_conv_b_o"]), "bkv3": bkv3,
         "w3kv": pair(i["L3_conv_w_k"], i["L3_conv_w_v"]).reshape(128, HEADS * 128)},
    ]


def build(nc, x, packs, out):
    f32, bf16 = mybir.dt.float32, mybir.dt.bfloat16
    ALU, ACT, AX = mybir.AluOpType, mybir.ActivationFunctionType, mybir.AxisListType
    x_v = x.rearrange("b (t a) w c -> b (a w) t c", t=TILES)
    out_v = out.rearrange("b (t a) w c -> b (a w) t c", t=TILES)

    ctx = ExitStack()
    with ctx:
        def sb(name, shape, dt=f32):
            return ctx.enter_context(nc.sbuf_tensor(name, shape, dt))

        def sem(name):
            return ctx.enter_context(nc.semaphore(name))

        CONST_F, CONST_B, W0, W12, W3 = range(5)
        packed = [sb(f"packed{n}", [128, ap.shape[1]], bf16 if n == CONST_B else f32) for n, (ap, _) in enumerate(packs)]
        part = {name: packed[n][:, a:b] for n, (_, where) in enumerate(packs) for name, (a, b) in where.items()}
        ident, group_avg, inv_count = part["ident"], part["group_avg"], part["inv_count"]
        pick_v = part["pick_v"][0:STRIP, :]
        mask_l, mask_r = part["mask_left"][0:BLK_ROWS + 1, :], part["mask_right"][0:BLK_ROWS + 1, :]
        chunk_of = part["chunk_of"][0:STRIP * PARTS, :]
        bkv3 = part["bkv3"][0:STRIP * PARTS, :]
        bkv3_parts = sb("bkv3_parts", [STRIP * PARTS, 128], bf16)
        w2g = sb("w2g", [128, C])

        x_in = [sb(f"x_in{g}", [128, TILES, C]) for g in range(IMAGES)]
        xT = [sb(f"xT{g}", [128, TOK]) for g in range(IMAGES)]
        qT = [sb(f"qT{g}", [128, 2, TOK]) for g in range(IMAGES)]
        v = [sb(f"v{g}", [128, TILES, C]) for g in range(IMAGES)]
        prob = [sb(f"prob{g}", [128, TILES, 512]) for g in range(IMAGES)]
        probT = [sb(f"probT{g}", [128, TILES, 512]) for g in range(IMAGES)]
        negmax = [sb(f"negmax{g}", [128, TILES, HEADS]) for g in range(IMAGES)]
        total = [sb(f"total{g}", [128, TILES]) for g in range(IMAGES)]
        inv = [sb(f"inv{g}", [128, TILES, HEADS]) for g in range(IMAGES)]
        stats = sb("stats", [128, IMAGES, 2, 3])
        means = sb("means", [128, IMAGES])
        spread = sb("spread", [128, IMAGES, 2])
        scale_gn, shift_gn = sb("scale_gn", [128, IMAGES]), sb("shift_gn", [128, IMAGES])
        var_gn, neg_half = sb("var_gn", [128, IMAGES]), sb("neg_half", [128, NORM_IMAGES])
        poolT = [sb(f"poolT{g}", [128, PSIDE, PSIDE]) for g in range(IMAGES)]
        kdiag = [sb(f"kdiag{g}", [128, STRIPS, HEADS * PTOK]) for g in range(IMAGES)]
        vdiag = [sb(f"vdiag{g}", [128, HEADS, 2, DH + 1]) for g in range(IMAGES)]
        q2v = [probT[g][:, 1, :] for g in range(IMAGES)]
        poolW = [prob[g][:, 0, 0:SIDE * PSIDE].rearrange("p (h w) -> p h w", w=PSIDE) for g in range(IMAGES)]
        o_tok, oT, y = v, [qT[g][:, 0, :] for g in range(IMAGES)], x_in
        bank = [ctx.enter_context(nc.psum_tensor(f"bank{b}", [128, 512], f32)) for b in range(BANKS)]

        order = [("xT", 0, g) for g in range(0, IMAGES, 2)]
        order += [(kind, 0, g) for g in range(0, IMAGES, NORM_IMAGES) for kind in ("group mean", "group var")]
        order += [("w2g", 2, 0)]
        for layer in range(3):
            kinds = (("qk",), ("v",)) if layer == 0 else (("qkv",),)
            for kind, in kinds + (("scores",), ("probT",), ("o",)):
                order += [(kind, layer, g) for g in range(IMAGES)]
        for kinds in (("kv", "q"), ("vd",), ("scores0", "scores1"), ("probT0", "probT1"), ("pv",), ("oT",), ("y",)):
            order += [(kind, 3, g) for g in range(IMAGES) for kind in kinds]
        place = {tile: n for n, tile in enumerate(order)}

        filled = [sem(f"filled{b}") for b in range(BANKS)]
        drained = [sem(f"drained{b}") for b in range(BANKS)]

        def psum(kind, layer, g=0):
            return bank[place[kind, layer, g] % BANKS]

        def filled_by(kind, layer, g=0):
            return filled[place[kind, layer, g] % BANKS], 1

        def drained_by(kind, layer, g=0):
            return drained[place[kind, layer, g] % BANKS], 1

        def count(kind, layer, g=0):
            return place[kind, layer, g] // BANKS + 1

        def wait_filled(eng, kind, layer, g=0):
            eng.wait_ge(filled[place[kind, layer, g] % BANKS], count(kind, layer, g))

        def wait_drained(eng, kind, layer, g=0):
            eng.wait_ge(drained[place[kind, layer, g] % BANKS], count(kind, layer, g))

        def view(ap, n):
            return ap.rearrange("p (n f) -> p n f", n=n)

        s_packed = [sem(f"packed_loaded{n}") for n in range(len(packs))]
        s_x = [sem(f"x_loaded{g}") for g in range(IMAGES)]
        s_y = sem("y_stored")
        s_half, s_zero, s_ones, s_bkv = sem("half_set"), sem("zeros_set"), sem("ones_set"), sem("kv_bias_step")
        s_gated, s_bias = sem("gates_applied"), sem("biases_scaled")
        s_norm, s_moments, s_rstd, s_factors, s_normed = (sem(n) for n in (
            "norm_step", "channel_moments", "inverse_deviations", "norm_factors", "x_normed"))
        s_qk1 = sem("qk1_ready")
        s_max, s_inv, s_scaled = sem("max_ready"), sem("inv_ready"), sem("prob_scaled")
        s_pool = sem("pool_step")
        s_strips, s_max3, s_exp3, s_inv3 = sem("kdiag_strips"), sem("max3_ready"), sem("exp3_ready"), sem("inv3_ready")

        def unit(layer, g):
            return layer * IMAGES + g + 1

        def keys_of(layer):
            return 128 if layer == 1 else TOK

        def scale_prob(dve, layer, g):
            wait_drained(dve, "scores", layer, g)
            nc.vector.reciprocal(inv[g][:, :, 0], total[g][:, :]).then_inc(s_inv, 1)
            dve.wait_ge(s_inv, unit(layer, g))
            for t in range(TILES):
                p = prob[g][:, t, 0:keys_of(layer)]
                last = nc.vector.tensor_scalar(p, p, inv[g][:, t, 0:1], None, ALU.mult)
            last.then_inc(s_scaled, 1)

        SCALE_LAG = 2
        POOL_STEPS = 5
        KV_BIAS_STEPS = 1 + PARTS * (PARTS - 1)
        DVE_STRIPS = 2
        block = ctx.enter_context(nc.Block())

        @block.sync
        def _(sp):
            for g in range(0, IMAGES, 2):
                sp.dma_start(x_in[g][:, :, :], x_v[g]).then_inc(s_x[g], 16)
                if g == 0:
                    sp.dma_start(packed[CONST_F][:, :], packs[CONST_F][0]).then_inc(s_packed[CONST_F], 16)
            sp.dma_start(packed[W12][:, :], packs[W12][0]).then_inc(s_packed[W12], 16)
            sp.dma_start(packed[CONST_B][:, :], packs[CONST_B][0]).then_inc(s_packed[CONST_B], 16)
            for g in range(IMAGES):
                wait_drained(sp, "y", 3, g)
                sp.dma_start(out_v[g], y[g][:, :, :]).then_inc(s_y, 16)
            sp.wait_ge(s_y, 16 * IMAGES)

        @block.gpsimd
        def _(pool):
            nc.gpsimd.memset(neg_half[:, :], -0.5).then_inc(s_half, 1)
            pool.wait_ge(s_half, 1)
            for n in range(IMAGES // NORM_IMAGES):
                wait_drained(pool, "group var", 0, n * NORM_IMAGES)
                at = slice(n * NORM_IMAGES, (n + 1) * NORM_IMAGES)
                nc.gpsimd.tensor_tensor(var_gn[:, at], var_gn[:, at], neg_half[:, :], ALU.pow).then_inc(s_rstd, 1)
            pool.wait_ge(s_packed[W12], 16)
            pool.wait_ge(s_packed[W0], 16)
            for w, gate in (("w1v", "gamma1"), ("w2v", "gamma2")):
                nc.gpsimd.tensor_scalar(part[w], part[w], part[gate], None, ALU.mult).then_inc(s_gated, 1)
            for g in range(IMAGES):
                nc.gpsimd.memset(vdiag[g][:, :, :, :], 0.0).then_inc(s_zero, 1)
            for g in range(IMAGES):
                nc.gpsimd.memset(kdiag[g][:, :, :], 0.0).then_inc(s_zero, 1)
            for g in range(IMAGES):
                wait_drained(pool, "o", 2, g)
                xi = xT[g][:, :].rearrange("p (h w) -> p h w", w=SIDE)
                w, p = poolW[g], poolT[g]
                first = g * POOL_STEPS
                nc.gpsimd.tensor_tensor(w[:, :, :], xi[:, :, 0::2], xi[:, :, 1::2], ALU.add).then_inc(s_pool, 1)
                pool.wait_ge(s_pool, first + 1)
                nc.gpsimd.tensor_tensor(w[:, :, 0:PSIDE - 1], w[:, :, 0:PSIDE - 1], xi[:, :, 2::2], ALU.add).then_inc(s_pool, 1)
                pool.wait_ge(s_pool, first + 2)
                nc.gpsimd.tensor_tensor(p[:, :, :], w[:, 0::2, :], w[:, 1::2, :], ALU.add).then_inc(s_pool, 1)
                pool.wait_ge(s_pool, first + 3)
                nc.gpsimd.tensor_tensor(p[:, 0:PSIDE - 1, :], p[:, 0:PSIDE - 1, :], w[:, 2::2, :], ALU.add).then_inc(s_pool, 1)
                pool.wait_ge(s_pool, first + 4)
                nc.gpsimd.tensor_tensor(p[:, :, :], p[:, :, :], view(inv_count, PSIDE), ALU.mult).then_inc(s_pool, 1)

        @block.scalar
        def _(act):
            for g in range(1, IMAGES, 2):
                act.dma_start(x_in[g][:, :, :], x_v[g]).then_inc(s_x[g], 16)
                if g == 3:
                    act.dma_start(packed[W0][:, :], packs[W0][0]).then_inc(s_packed[W0], 16)
            act.dma_start(packed[W3][:, :], packs[W3][0]).then_inc(s_packed[W3], 16)
            for g in range(IMAGES):
                wait_filled(act, "xT", 0, g - g % 2)
                act.wait_ge(s_factors, g // NORM_IMAGES + 1)
                last = nc.scalar.activation(xT[g][:, :], view(psum("xT", 0, g - g % 2)[:, :], 2)[:, g % 2, :], ACT.Identity,
                                            bias=shift_gn[:, g:g + 1], scale=scale_gn[:, g:g + 1])
                last.then_inc(*(drained_by("xT", 0, g - 1) if g % 2 else (s_normed, 1)))
            for layer in range(3):
                kind = "v" if layer == 0 else "qkv"
                keys = keys_of(layer)
                for g in range(IMAGES):
                    wait_filled(act, kind, layer, g)
                    ps = psum(kind, layer, g)
                    if layer == 0:
                        last = nc.scalar.activation(v[g][:, :, :], view(ps[:, 0:TOK], TILES), ACT.Copy)
                    elif layer == 1:
                        act.wait_ge(s_qk1, g + 1)
                        last = nc.scalar.activation(v[g][:, :, :], view(ps[:, TOK:], TILES), ACT.Copy)
                    else:
                        last = nc.scalar.activation(q2v[g], ps[:, :], ACT.Copy)
                    last.then_inc(*drained_by(kind, layer, g))
                for g in range(IMAGES):
                    act.wait_ge(s_max, unit(layer, g))
                    for t in range(TILES):
                        last = nc.scalar.activation(prob[g][:, t, 0:keys], psum("scores", layer, g)[:, keys * t:keys * t + keys],
                                                    ACT.Exp, bias=negmax[g][:, t, 0:1], accum_out=total[g][:, t:t + 1])
                    last.then_inc(*drained_by("scores", layer, g))
                for g in range(IMAGES):
                    wait_filled(act, "probT", layer, g)
                    nc.scalar.activation(probT[g][:, 0, 0:TILES * keys], psum("probT", layer, g)[:, 0:TILES * keys], ACT.Copy)\
                        .then_inc(*drained_by("probT", layer, g))
            act.wait_ge(s_zero, 2 * IMAGES)
            act.wait_ge(s_bias, 2)
            for g in range(IMAGES):
                wait_filled(act, "kv", 3, g)
                for b in range(DVE_STRIPS, STRIPS):
                    at = slice(STRIP * b, STRIP * b + STRIP)
                    if b == STRIPS - 1:
                        act.wait_ge(s_strips, g + 1)
                    last = nc.scalar.activation(kdiag[g][at, b, :], psum("kv", 3, g)[at, :], ACT.Copy)
                last.then_inc(*drained_by("kv", 3, g))
                wait_filled(act, "q", 3, g)
                for a in range(HALVES):
                    last = nc.scalar.activation(qT[g][:, a, :], psum("q", 3, g)[:, TOK * a:TOK * a + TOK], ACT.Identity,
                                                bias=part["bq3"][:, a:a + 1], scale=float(DH) ** -0.5)
                last.then_inc(*drained_by("q", 3, g))
            for g in range(IMAGES):
                wait_filled(act, "vd", 3, g)
                for c2 in range(2):
                    at = slice(KEYS * c2, KEYS * c2 + KEYS)
                    last = nc.scalar.activation(vdiag[g][at, :, c2, 0:DH], view(psum("vd", 3, g)[at, 0:C], HEADS), ACT.Copy)
                last.then_inc(*drained_by("vd", 3, g))
            for g in range(IMAGES):
                for t in range(TILES):
                    wait_drained(act, f"scores{t}", 3, g)
                    nc.scalar.activation(prob[g][:, t, :], prob[g][:, t, :], ACT.Exp).then_inc(s_exp3, 1)
            for g in range(IMAGES):
                for t in range(TILES):
                    wait_filled(act, f"probT{t}", 3, g)
                    nc.scalar.activation(probT[g][:, t, :], psum(f"probT{t}", 3, g)[:, :], ACT.Copy)\
                        .then_inc(*drained_by(f"probT{t}", 3, g))
            for g in range(IMAGES):
                wait_filled(act, "oT", 3, g)
                nc.scalar.activation(oT[g], psum("oT", 3, g)[:, 0:TOK], ACT.Copy).then_inc(*drained_by("oT", 3, g))

        @block.vector
        def _(dve):
            steps = [0]

            def link(ins):
                ins.then_inc(s_norm, 1)
                steps[0] += 1
                dve.wait_ge(s_norm, steps[0])

            for g in range(IMAGES):
                wait_filled(dve, "xT", 0, g - g % 2)
                nc.vector.bn_stats(stats[:, g, :, :], view(psum("xT", 0, g - g % 2)[:, :], 2)[:, g % 2, :]).then_inc(s_moments, 1)
            for n in range(IMAGES // NORM_IMAGES):
                g, at = n * NORM_IMAGES, slice(n * NORM_IMAGES, (n + 1) * NORM_IMAGES)
                wait_filled(dve, "group mean", 0, g)
                link(nc.vector.tensor_scalar(means[:, at], psum("group mean", 0, g)[:, 0:NORM_IMAGES], 0.5, None, ALU.mult))
                link(nc.vector.tensor_tensor(spread[:, at, :], stats[:, at, :, 1],
                                             means[:, at].unsqueeze(2).broadcast_to([128, NORM_IMAGES, 2]), ALU.subtract))
                link(nc.vector.tensor_tensor(spread[:, at, :], spread[:, at, :], spread[:, at, :], ALU.mult))
                nc.vector.scalar_tensor_tensor(out=spread[:, at, :], in0=stats[:, at, :, 2], scalar=2.0 / TOK, in1=spread[:, at, :],
                                               op0=ALU.mult, op1=ALU.add).then_inc(*drained_by("group mean", 0, g))
                wait_filled(dve, "group var", 0, g)
                nc.vector.tensor_scalar(var_gn[:, at], psum("group var", 0, g)[:, 0:NORM_IMAGES], 0.5, GN_EPS, ALU.mult, ALU.add)\
                    .then_inc(*drained_by("group var", 0, g))
                dve.wait_ge(s_packed[W0], 16)
                dve.wait_ge(s_rstd, n + 1)
                link(nc.vector.tensor_scalar(scale_gn[:, at], var_gn[:, at], part["gn_gamma"], None, ALU.mult))
                link(nc.vector.tensor_tensor(means[:, at], means[:, at], scale_gn[:, at], ALU.mult))
                nc.vector.tensor_scalar(shift_gn[:, at], means[:, at], -1.0, part["gn_beta"], ALU.mult, ALU.add).then_inc(s_factors, 1)
            nc.vector.tensor_scalar(part["bv1"], part["bv1"], part["gamma1"], None, ALU.mult).then_inc(s_bias, 1)
            dve.wait_ge(s_packed[W3], 16)
            nc.vector.tensor_scalar(part["bq3"], part["bq3"], float(DH) ** -0.5, None, ALU.mult).then_inc(s_bias, 1)
            wait_filled(dve, "w2g", 2)
            nc.vector.tensor_copy(w2g[:, :], psum("w2g", 2)[:, 0:C]).then_inc(*drained_by("w2g", 2))
            nc.vector.tensor_copy(bkv3_parts[:, :], bkv3).then_inc(s_bkv, 1)
            done = 1
            for k in range(1, PARTS):
                for at in (slice(STRIP * p, STRIP * p + STRIP) for p in range(k, PARTS)):
                    dve.wait_ge(s_bkv, done)
                    nc.vector.tensor_tensor(bkv3[at], bkv3[at], bkv3_parts[at, :], ALU.subtract).then_inc(s_bkv, 1)
                    dve.wait_ge(s_bkv, done + 1)
                    nc.vector.tensor_copy(bkv3_parts[at, :], bkv3[at]).then_inc(s_bkv, 1)
                    done += 2
            assert done == KV_BIAS_STEPS
            dve.wait_ge(s_bias, 2)
            for layer in range(3):
                keys = keys_of(layer)
                if layer < 2:
                    kind = ("qk", "qkv")[layer]
                    for g in range(IMAGES):
                        wait_filled(dve, kind, layer, g)
                        ps = psum(kind, layer, g)
                        if layer == 0:
                            nc.vector.tensor_scalar(qT[g][:, 0, :], ps[:, 0:TOK], part["bq0"], float(C) ** -0.5, ALU.add, ALU.mult)
                            nc.vector.tensor_scalar(qT[g][:, 1, :], ps[:, TOK:], part["bk0"], None, ALU.add)\
                                .then_inc(*drained_by("qk", layer, g))
                        else:
                            nc.vector.tensor_scalar(qT[g][0:DQK, 0, :], ps[0:DQK, 0:TOK], part["bq1"][0:DQK], 0.0, ALU.add, ALU.max)
                            nc.vector.tensor_scalar(qT[g][0:DQK, 1, :], ps[STRIP:STRIP + DQK, 0:TOK], part["bk1"][0:DQK], 0.0,
                                                    ALU.add, ALU.max).then_inc(s_qk1, 1)
                for g in range(IMAGES):
                    wait_filled(dve, "scores", layer, g)
                    nc.vector.tensor_reduce(out=negmax[g][:, :, 0], in_=view(psum("scores", layer, g)[:, 0:TILES * keys], TILES),
                                            op=ALU.max, axis=AX.X, negate=True).then_inc(s_max, 1)
                    if g >= SCALE_LAG:
                        scale_prob(dve, layer, g - SCALE_LAG)
                for g in range(IMAGES - SCALE_LAG, IMAGES):
                    scale_prob(dve, layer, g)
                for g in range(IMAGES):
                    wait_filled(dve, "o", layer, g)
                    ps = psum("o", layer, g)[:, 0:TOK]
                    if layer < 2:
                        last = nc.vector.scalar_tensor_tensor(out=xT[g][:, :], in0=ps, scalar=part[("bv0", "bv1")[layer]],
                                                              in1=xT[g][:, :], op0=ALU.add, op1=ALU.add)
                    else:
                        last = nc.vector.tensor_tensor(xT[g][:, :], ps, xT[g][:, :], ALU.add)
                    last.then_inc(*drained_by("o", layer, g))
            dve.wait_ge(s_zero, 2 * IMAGES)
            for g in range(IMAGES):
                for c2 in range(2):
                    nc.vector.memset(vdiag[g][KEYS * c2:KEYS * c2 + KEYS, :, c2, DH:DH + 1], 1.0).then_inc(s_ones, 1)
                wait_filled(dve, "kv", 3, g)
                for b in range(DVE_STRIPS):
                    at = slice(STRIP * b, STRIP * b + STRIP)
                    last = nc.vector.tensor_copy(kdiag[g][at, b, :], psum("kv", 3, g)[at, :])
                last.then_inc(s_strips, 1)
            for g in range(IMAGES):
                for t in range(TILES):
                    wait_filled(dve, f"scores{t}", 3, g)
                    s3 = view(psum(f"scores{t}", 3, g)[:, :], HEADS)
                    nc.vector.tensor_reduce(out=negmax[g][:, t, :], in_=s3, op=ALU.max, axis=AX.X, negate=True).then_inc(s_max3, 1)
                    dve.wait_ge(s_max3, TILES * g + t + 1)
                    nc.vector.tensor_tensor(view(prob[g][:, t, :], HEADS), s3,
                                            negmax[g][:, t, :].unsqueeze(2).broadcast_to([128, HEADS, KEYS]), ALU.add)\
                        .then_inc(*drained_by(f"scores{t}", 3, g))
            for g in range(IMAGES):
                wait_filled(dve, "pv", 3, g)
                pv = psum("pv", 3, g)[:, 0:TILES * HEADS * (DH + 1)].rearrange("p (c e) -> p c e", e=DH + 1)
                inv3 = inv[g][:, :, :].rearrange("p t c -> p (t c)")
                nc.vector.reciprocal(inv3, pv[:, :, DH]).then_inc(s_inv3, 1)
                dve.wait_ge(s_inv3, g + 1)
                nc.vector.tensor_tensor(o_tok[g][:, :, :].rearrange("p t (c d) -> p (t c) d", d=DH), pv[:, :, 0:DH],
                                        inv3.unsqueeze(2).broadcast_to([128, TILES * HEADS, DH]), ALU.mult)\
                    .then_inc(*drained_by("pv", 3, g))
            for g in range(IMAGES):
                wait_filled(dve, "y", 3, g)
                nc.vector.tensor_tensor(y[g][:, :, :], view(psum("y", 3, g)[:, 0:TOK], TILES),
                                        part["bo3"].unsqueeze(1).broadcast_to([128, TILES, C]), ALU.add)\
                    .then_inc(*drained_by("y", 3, g))

        @block.tensor
        def _(pe):
            mm, transpose = nc.tensor.matmul, nc.tensor.transpose

            def begin(kind, layer, g=0):
                b, n = place[kind, layer, g] % BANKS, count(kind, layer, g)
                if n > 1:
                    pe.wait_ge(drained[b], n - 1)
                return bank[b]

            pe.wait_ge(s_packed[CONST_F], 16)
            for g in range(IMAGES):
                pe.wait_ge(s_x[g], 16)
                ps = begin("xT", 0, g - g % 2)
                for t in range(TILES):
                    last = transpose(view(ps[:, :], 2)[:, g % 2, 128 * t:128 * t + 128], x_in[g][:, t, :], ident)
                if g % 2:
                    last.then_inc(*filled_by("xT", 0, g - 1))
            for g in range(0, IMAGES, NORM_IMAGES):
                pe.wait_ge(s_moments, g + NORM_IMAGES)
                ps = begin("group mean", 0, g)
                for half in range(2):
                    last = mm(ps[:, 0:NORM_IMAGES], group_avg, stats[:, g:g + NORM_IMAGES, half, 1], start=half == 0, stop=half == 1)
                last.then_inc(*filled_by("group mean", 0, g))
                wait_drained(pe, "group mean", 0, g)
                ps = begin("group var", 0, g)
                for half in range(2):
                    last = mm(ps[:, 0:NORM_IMAGES], group_avg, spread[:, g:g + NORM_IMAGES, half], start=half == 0, stop=half == 1)
                last.then_inc(*filled_by("group var", 0, g))
            pe.wait_ge(s_packed[W12], 16)
            turned = part["w2qk_turned"][0:DQK, :]
            mm(begin("w2g", 2)[:, 0:C], turned[:, 0:C], turned[:, C:], start=True, stop=True).then_inc(*filled_by("w2g", 2))
            pe.wait_ge(s_packed[W0], 16)
            for layer in range(3):
                keys = keys_of(layer)
                wv = part[("w0v", "w1v", "w2v")[layer]]
                kind = "qk" if layer == 0 else "qkv"
                if layer == 1:
                    pe.wait_ge(s_packed[CONST_B], 16)
                    pe.wait_ge(s_gated, 2)
                if layer == 2:
                    wait_drained(pe, "w2g", 2)
                for g in range(IMAGES):
                    if layer == 0 and g % 2 == 0:
                        pe.wait_ge(s_normed, g // 2 + 1)
                    elif layer == 0:
                        wait_drained(pe, "xT", 0, g - 1)
                    else:
                        wait_drained(pe, "o", layer - 1, g)
                    ps = begin(kind, layer, g)
                    if layer == 0:
                        mm(ps[:, 0:TOK], part["w0q"], xT[g][:, :], start=True, stop=True)
                        mm(ps[:, TOK:], part["w0k"], xT[g][:, :], start=True, stop=True).then_inc(*filled_by(kind, layer, g))
                    else:
                        if layer == 1:
                            mm(ps[0:64, 0:TOK], part["w1qk"], xT[g][:, :], start=True, stop=True)
                        else:
                            mm(ps[:, 0:TOK], w2g[:, :], xT[g][:, :], start=True, stop=True)
                        for t in range(TILES):
                            last = mm(ps[:, TOK + C * t:TOK + C * t + C], xT[g][:, 128 * t:128 * t + 128], wv, start=True, stop=True)
                        last.then_inc(*filled_by(kind, layer, g))
                if layer == 0:
                    for g in range(IMAGES):
                        ps = begin("v", layer, g)
                        for t in range(TILES):
                            last = mm(ps[:, C * t:C * t + C], xT[g][:, 128 * t:128 * t + 128], wv, start=True, stop=True)
                        last.then_inc(*filled_by("v", layer, g))
                for g in range(IMAGES):
                    if layer == 1:
                        pe.wait_ge(s_qk1, g + 1)
                    else:
                        wait_drained(pe, kind, layer, g)
                    q = (qT[g][:, 0, :], qT[g][0:DQK, 0, :], q2v[g][:, 0:TOK])[layer]
                    k = (qT[g][:, 1, :], qT[g][0:DQK, 1, :], xT[g][:, :])[layer]
                    ps = begin("scores", layer, g)
                    for t in range(TILES):
                        at = slice(128 * t, 128 * t + 128)
                        if layer == 1:
                            mm(ps[:, at], q[:, at], k[:, at], start=True, stop=False)
                            last = mm(ps[:, at], mask_l, mask_r, start=False, stop=True)
                        else:
                            last = mm(ps[:, TOK * t:TOK * t + TOK], q[:, at], k, start=True, stop=True)
                    last.then_inc(*filled_by("scores", layer, g))
                for g in range(IMAGES):
                    pe.wait_ge(s_scaled, unit(layer, g))
                    ps = begin("probT", layer, g)
                    for k in range(keys // 128):
                        for t in range(TILES):
                            last = transpose(ps[:, TOK * k + 128 * t:TOK * k + 128 * t + 128], prob[g][:, t, 128 * k:128 * k + 128], ident)
                    last.then_inc(*filled_by("probT", layer, g))
                for g in range(IMAGES):
                    wait_drained(pe, "v" if layer == 0 else kind, layer, g)
                    wait_drained(pe, "probT", layer, g)
                    vals = q2v[g][:, TOK:].rearrange("p (t c) -> p t c", c=C) if layer == 2 else v[g][:, :, :]
                    ps = begin("o", layer, g)
                    if layer == 1:
                        for t in range(TILES):
                            last = mm(ps[:, 128 * t:128 * t + 128], vals[:, t, :], probT[g][:, 0, 128 * t:128 * t + 128],
                                      start=True, stop=True)
                    else:
                        for k in range(TILES):
                            last = mm(ps[:, 0:TOK], vals[:, k, :], probT[g][:, 0, TOK * k:TOK * k + TOK], start=k == 0, stop=k == TILES - 1)
                    last.then_inc(*filled_by("o", layer, g))
            pe.wait_ge(s_packed[W3], 16)
            pe.wait_ge(s_bkv, KV_BIAS_STEPS)
            for g in range(IMAGES):
                pe.wait_ge(s_pool, (g + 1) * POOL_STEPS)
                ps = begin("kv", 3, g)
                mm(ps[:, :], bkv3_parts[:, :], chunk_of, start=True, stop=False, skip_group_check=True)
                for c in range(HEADS):
                    last = mm(ps[:, :].rearrange("p (j c m) -> p j c m", j=HEADS, c=HEADS)[:, :, c, :],
                              part["w3kv"][:, 128 * c:128 * c + 128], poolT[g][:, :, :], start=False, stop=c == HEADS - 1,
                              skip_group_check=True)
                last.then_inc(*filled_by("kv", 3, g))
                ps = begin("q", 3, g)
                for a in range(HALVES):
                    last = mm(ps[:, TOK * a:TOK * a + TOK], part["w3q"][:, 128 * a:128 * a + 128], xT[g][:, :], start=True, stop=True)
                last.then_inc(*filled_by("q", 3, g))
            for g in range(IMAGES):
                wait_drained(pe, "kv", 3, g)
                ps = begin("vd", 3, g)
                for j in range(HEADS):
                    for c2 in range(2):
                        last = mm(ps[KEYS * c2:KEYS * c2 + KEYS, DH * j:DH * j + DH], kdiag[g][0:STRIP, 0, KEYS * j:KEYS * j + KEYS],
                                  pick_v, start=True, stop=True)
                last.then_inc(*filled_by("vd", 3, g))
            for g in range(IMAGES):
                wait_drained(pe, "q", 3, g)
                for t in range(TILES):
                    ps = begin(f"scores{t}", 3, g)
                    for a in range(HALVES):
                        for s in range(STRIPS):
                            j = STRIPS * t + s
                            last = mm(view(ps[STRIP * s:STRIP * s + STRIP, TOK * a:TOK * a + TOK], STRIPS),
                                      qT[g][:, a, HTOK * j:HTOK * j + HTOK], kdiag[g][:, :, KEYS * j:KEYS * j + KEYS],
                                      start=True, stop=True)
                    last.then_inc(*filled_by(f"scores{t}", 3, g))
            for g in range(IMAGES):
                for t in range(TILES):
                    pe.wait_ge(s_exp3, TILES * g + t + 1)
                    ps = begin(f"probT{t}", 3, g)
                    for p in range(PAIRS):
                        last = transpose(ps[:, 128 * p:128 * p + 128], prob[g][:, t, 128 * p:128 * p + 128], ident)
                    last.then_inc(*filled_by(f"probT{t}", 3, g))
            pe.wait_ge(s_ones, 2 * IMAGES)
            for g in range(IMAGES):
                wait_drained(pe, "vd", 3, g)
                ps = begin("pv", 3, g)
                for t in range(TILES):
                    wait_drained(pe, f"probT{t}", 3, g)
                    for p in range(PAIRS):
                        for s in range(STRIPS):
                            at = (t * PAIRS + p) * 2 * (DH + 1)
                            last = mm(ps[STRIP * s:STRIP * s + STRIP, at:at + 2 * (DH + 1)],
                                      probT[g][:, t, 128 * p + STRIP * s:128 * p + STRIP * s + STRIP],
                                      vdiag[g][:, STRIPS * t + s, :, :].rearrange("p c e -> p (c e)"), start=True, stop=True)
                last.then_inc(*filled_by("pv", 3, g))
            for g in range(IMAGES):
                wait_drained(pe, "pv", 3, g)
                ps = begin("oT", 3, g)
                for t in range(TILES):
                    last = transpose(ps[:, 128 * t:128 * t + 128], o_tok[g][:, t, :], ident)
                last.then_inc(*filled_by("oT", 3, g))
            for g in range(IMAGES):
                wait_drained(pe, "oT", 3, g)
                ps = begin("y", 3, g)
                for t in range(TILES):
                    mm(ps[:, C * t:C * t + C], oT[g][:, 128 * t:128 * t + 128], part["w3o"], start=True, stop=False)
                    last = mm(ps[:, C * t:C * t + C], xT[g][:, 128 * t:128 * t + 128], ident, start=False, stop=True)
                last.then_inc(*filled_by("y", 3, g))


def kernel(**inputs):
    import numpy as _np
    import ml_dtypes as _mld
    import concourse.bacc as _bacc
    from concourse import mybir as _mybir
    from concourse.bass_utils import run_bass_kernel_spmd as _run

    nc = _bacc.Bacc("TRN2", target_bir_lowering=False, num_devices=1)
    inputs = {k: _np.asarray(v) for k, v in inputs.items()}
    arrays = {"in_x_dram": _np.ascontiguousarray(inputs["x"])}
    groups = [*constants(), *arrange(inputs)]
    packs = []
    for n, group in enumerate(groups):
        where, at = {}, 0
        for name, a in group.items():
            where[name] = (at, at + a.shape[1])
            at += a.shape[1]
        a = _np.ascontiguousarray(_np.concatenate(list(group.values()), axis=1))
        if n == 1:
            a = a.astype(_mld.bfloat16)
        arrays[f"in_pack{n}_dram"] = a
        packs.append((nc.dram_tensor(f"in_pack{n}_dram", a.shape, _mybir.dt.from_np(a.dtype), kind="ExternalInput").ap(), where))
    x = nc.dram_tensor("in_x_dram", inputs["x"].shape, _mybir.dt.float32, kind="ExternalInput").ap()
    out = nc.dram_tensor("out_0_dram", (IMAGES, SIDE, SIDE, C), _mybir.dt.float32, kind="ExternalOutput").ap()
    build(nc, x, packs, out)
    r = _run(nc, [arrays], core_ids=[0])
    return r.results[0]["out_0_dram"]
```

```python
import numpy as np
import concourse.bass as bass
from concourse import mybir
from contextlib import ExitStack

IMAGES, SIDE, C = 8, 16, 128
TOK = SIDE * SIDE
TILES = TOK // 128
GROUPS = 16
GN_EPS = 1e-3
DQK = C // 8
HEADS, DH = 8, 16
PSIDE = SIDE // 2
PTOK = PSIDE * PSIDE
HKEY = PTOK // HEADS
KEYS = HKEY * HEADS
STRIPS, STRIP = 4, 32
HALVES = HEADS // STRIPS
HTOK = TOK // HEADS
PAIRS = HEADS // 2
BANKS = 8
MASK_ROWS = STRIP // SIDE + 1
HALF = IMAGES // 2
BIG = float(2 ** 100)


def constants():
    n = np.full(PSIDE, 3.0)
    n[-1] = 2.0
    f = {"ident": np.eye(128), "group_avg": np.kron(np.eye(GROUPS), np.full((C // GROUPS,) * 2, 0.5 * GROUPS / C)),
         "inv_count": np.broadcast_to((1.0 / np.outer(n, n)).reshape(1, PTOK), (128, PTOK))}
    left, right = np.zeros((128, 128)), np.zeros((128, TILES * STRIP))
    rows = np.kron(np.eye(STRIP // SIDE), np.ones((1, SIDE)))
    left[:MASK_ROWS - 1], left[MASK_ROWS - 1] = np.tile(rows, STRIPS), 1.0
    right[:MASK_ROWS - 1], right[MASK_ROWS - 1] = np.tile(rows, TILES) * BIG, -BIG
    b = {"mask_left": left, "mask_right": right}
    return {k: v.astype(np.float32) for k, v in f.items()}, {k: v.astype(np.float32) for k, v in b.items()}


def arrange(i):
    def column(v):
        out = np.zeros((128, 1), np.float32)
        out[:v.shape[0], 0] = v
        return out

    def everywhere(v):
        return np.broadcast_to(v.reshape(1, -1), (128, v.size))

    def strips(w):
        out = np.zeros((w.shape[0], HEADS, STRIP), np.float32)
        out[:, :, 0:DH] = w.reshape(-1, HEADS, DH)
        return out.reshape(w.shape[0], HALVES * 128)

    def pair(k, v):
        both = np.stack([k.reshape(-1, HEADS, DH), v.reshape(-1, HEADS, DH)], axis=2)
        return np.repeat(both[:, :, None], STRIPS, axis=2)

    def strip(w):
        return np.concatenate([w, np.zeros((w.shape[0], STRIP - w.shape[1]), np.float32)], axis=1)

    bq3 = strips(i["L3_conv_b_q"].reshape(1, C)).reshape(HALVES, 128)
    bkv3 = pair(i["L3_conv_b_k"], i["L3_conv_b_v"]).reshape(HEADS, 128).T
    return [
        {"w0q": i["L0_conv_wq"], "w0k": i["L0_conv_wk"], "w0v": i["L0_conv_wv"],
         "gn_gamma": column(i["L0_conv_gn_gamma"]), "gn_beta": column(i["L0_conv_gn_beta"]),
         "bq0": column(i["L0_conv_bq"]), "bk0": column(i["L0_conv_bk"]), "bv0": column(i["L0_conv_bv"]),
         "bq1": column(i["L1_conv_bq"]), "bk1": column(i["L1_conv_bk"]), "bv1": column(i["L1_conv_bv"]),
         "gamma1": everywhere(i["L1_conv_gamma"]), "gamma2": everywhere(i["L2_conv_gamma"]), "bq3": bq3.T},
        {"w1q": strip(i["L1_conv_Wq"]), "w1k": strip(i["L1_conv_Wk"]), "w1v": i["L1_conv_Wv"],
         "w2q": strip(i["L2_conv_Wb"]), "w2k": strip(i["L2_conv_Wc"]), "w2v": i["L2_conv_Wd"]},
        {"w3q": strips(i["L3_conv_w_q"]), "w3o": i["L3_conv_w_o"], "bo3": column(i["L3_conv_b_o"]), "bkv3": bkv3,
         "w3kv": pair(i["L3_conv_w_k"], i["L3_conv_w_v"]).reshape(128, HEADS * 128)},
    ]


def build(nc, x, packs, out):
    f32, bf16 = mybir.dt.float32, mybir.dt.bfloat16
    ALU, ACT, AX = mybir.AluOpType, mybir.ActivationFunctionType, mybir.AxisListType
    x_v = x.rearrange("b (t a) w c -> (a w) b t c", t=TILES)
    out_v = out.rearrange("b (t a) w c -> b (a w) t c", t=TILES)

    ctx = ExitStack()
    with ctx:
        def sb(name, shape, dt=f32):
            return ctx.enter_context(nc.sbuf_tensor(name, shape, dt))

        def sem(name):
            return ctx.enter_context(nc.semaphore(name))

        CONST_F, CONST_B, W0, W12, W3 = range(5)
        packed = [sb(f"packed{n}", [128, ap.shape[1]], bf16 if n == CONST_B else f32) for n, (ap, _) in enumerate(packs)]
        part = {name: packed[n][:, a:b] for n, (_, where) in enumerate(packs) for name, (a, b) in where.items()}
        ident, group_avg, inv_count = part["ident"], part["group_avg"], part["inv_count"]
        mask_l, mask_r = part["mask_left"][0:MASK_ROWS, :], part["mask_right"][0:MASK_ROWS, :]

        x_all = sb("x_all", [128, IMAGES, TILES, C])
        x_in = [x_all[:, g] for g in range(IMAGES)]
        xT = [sb(f"xT{g}", [128, TOK]) for g in range(IMAGES)]
        qT = [sb(f"qT{g}", [128, 2, TOK]) for g in range(IMAGES)]
        v = [sb(f"v{g}", [128, TILES, C]) for g in range(IMAGES)]
        prob = [sb(f"prob{g}", [128, TILES, 512]) for g in range(IMAGES)]
        probT = [sb(f"probT{g}", [128, TILES, 512]) for g in range(IMAGES)]
        negmax = [sb(f"negmax{g}", [128, TILES, HEADS]) for g in range(IMAGES)]
        total = [sb(f"total{g}", [128, TILES]) for g in range(IMAGES)]
        inv = [sb(f"inv{g}", [128, TILES, HEADS]) for g in range(IMAGES)]
        stats = sb("stats", [128, IMAGES, 2, 3])
        means = sb("means", [128, IMAGES])
        spread = sb("spread", [128, IMAGES, 2])
        scale_gn, shift_gn = sb("scale_gn", [128, IMAGES]), sb("shift_gn", [128, IMAGES])
        var_gn, neg_half = sb("var_gn", [128, IMAGES]), sb("neg_half", [128, HALF])
        warm, warm_up = sb("warm", [128, 1]), sb("warm_up", [128, TOK], bf16)
        poolT = [sb(f"poolT{i}", [128, 2, PSIDE, PSIDE]) for i in range(IMAGES // 2)]
        kdiag = [sb(f"kdiag{i}", [128, STRIPS, 2 * HEADS * KEYS]) for i in range(IMAGES // 2)]
        vdiag = [sb(f"vdiag{i}", [128, 2 * HEADS, 2, DH]) for i in range(IMAGES // 2)]
        windows = [probT[g][:, 1, 0:TOK].rearrange("p (t q) -> p t q", t=TILES) for g in range(IMAGES)]
        poolW = [prob[g][:, 0, 0:SIDE * PSIDE].rearrange("p (h w) -> p h w", w=PSIDE) for g in range(IMAGES)]
        oT, y, xb = [qT[g][:, 0, :] for g in range(IMAGES)], x_in, [qT[g][:, 1, :] for g in range(IMAGES)]
        bank = [ctx.enter_context(nc.psum_tensor(f"bank{b}", [128, 512], f32)) for b in range(BANKS)]

        steps = [("norm", 0, 0), ("qk", 0, 4), ("v", 0, 3), ("scores", 0, 3), ("scale", 0, 2), ("probT", 0, 3), ("o", 0, 6)]
        steps += [("qk", 1, 1), ("v", 1, 1), ("scores", 1, 2), ("turn", 1, 2), ("o", 1, 2)]
        steps += [("qk", 2, 1), ("v", 2, 1), ("scores", 2, 3), ("scale", 2, 2), ("probT", 2, 2), ("o", 2, 2)]
        steps += [("pool", 3, 1), ("kv", 3, 3), ("q", 3, 3), ("vd", 3, 1), ("scores3", 3, 1), ("share3", 3, 2), ("probT3", 3, 2),
                  ("xb", 3, 1), ("pv", 3, 1), ("x", 3, 2), ("y", 3, 6)]
        due, start = [], 0
        for n, (kind, layer, distance) in enumerate(steps):
            start += distance
            for g in range(IMAGES):
                if kind not in ("kv", "vd") and (kind, layer) not in (("qk", 1), ("qk", 2)):
                    due.append((start + g, -n, kind, layer, g))
                elif g % 2:
                    due.append((start + g, -n, kind, layer, g - 1))
        sequence = [task[2:] for task in sorted(due)]
        sequence.insert(sequence.index(("qk", 1, 0)), ("setup", 1, 0))
        sequence.insert(sequence.index(("qk", 0, 1)), ("group var", 0, HALF))

        order = [("xT", 0, 0), ("xT", 0, 2)]
        order += [("xT", 0, 4), ("group mean", 0, 0), ("xT", 0, 6), ("group var", 0, 0)]
        order += [("group mean", 0, HALF)]
        parts_of = {"kv": ("kv0", "kv1"), "scores3": ("scores0", "scores1"), "probT3": ("probT0", "probT1"),
                    "norm": (), "scale": (), "turn": (), "pool": (), "setup": (), "xb": (), "share3": ()}
        for step, layer, g in sequence:
            order += [(kind, layer, g) for kind in parts_of.get(step, (step,))]
        place = {tile: n for n, tile in enumerate(order)}

        filled = [sem(f"filled{b}") for b in range(BANKS)]
        drained = [sem(f"drained{b}") for b in range(BANKS)]

        def psum(kind, layer, g=0):
            return bank[place[kind, layer, g] % BANKS]

        def filled_by(kind, layer, g=0):
            return filled[place[kind, layer, g] % BANKS], 1

        def drained_by(kind, layer, g=0):
            return drained[place[kind, layer, g] % BANKS], 1

        def count(kind, layer, g=0):
            return place[kind, layer, g] // BANKS + 1

        def wait_filled(eng, kind, layer, g=0):
            eng.wait_ge(filled[place[kind, layer, g] % BANKS], count(kind, layer, g))

        def wait_drained(eng, kind, layer, g=0):
            eng.wait_ge(drained[place[kind, layer, g] % BANKS], count(kind, layer, g))

        def view(ap, n):
            return ap.rearrange("p (n f) -> p n f", n=n)

        s_packed = [sem(f"packed_loaded{n}") for n in range(len(packs))]
        s_x = [sem(f"x_loaded{g}") for g in range(IMAGES)]
        s_y = sem("y_stored")
        s_warm, s_half, s_zero = sem("warm_up_set"), sem("half_set"), sem("zeros_set")
        s_gated, s_bias = sem("gates_applied"), sem("biases_scaled")
        s_norm, s_moments, s_rstd, s_factors, s_normed = (sem(n) for n in (
            "norm_step", "channel_moments", "inverse_deviations", "norm_factors", "x_normed"))
        s_windows, s_turn = sem("windows_cleared"), sem("window_step")
        s_max, s_inv, s_scaled0, s_scaled1 = (sem(n) for n in ("max_ready", "inv_ready", "prob0_scaled", "prob1_scaled"))
        s_strips_act = sem("kdiag_strips_by_scalar")
        s_pool, s_xb = sem("pool_step"), sem("output_bias_added")
        s_strips, s_max3, s_exp3, s_inv3, s_share3 = (sem(n) for n in (
            "kdiag_strips_by_vector", "max3_ready", "exp3_ready", "inv3_step", "prob3_scaled"))

        def nth(step, layer, g):
            return [(s, l, n) for s, l, n in sequence if s == step].index((step, layer, g)) + 1

        def keys_of(layer):
            return STRIP if layer == 1 else TOK

        def kv_strip(g, k, b):
            at, half = slice(STRIP * b, STRIP * b + STRIP), HEADS // 2
            to = kdiag[g // 2][at, b, :].rearrange("p (j c m) -> p c j m", c=HEADS, m=HKEY)[:, half * k:half * k + half, :, :]
            return to, prob[g + k][at, 1, :].rearrange("p (c j m) -> p c j m", c=half, m=HKEY)

        POOL_STEPS, TURN_STEPS = 5, 3
        DVE_STRIPS = 1
        EARLY, LATE = 2, 2
        block = ctx.enter_context(nc.Block())

        def clear_kdiag(eng, g):
            at = slice(g % 2 * HEADS * KEYS, (g % 2 + 1) * HEADS * KEYS)
            eng.memset(kdiag[g // 2][:, :, at], 0.0).then_inc(s_zero, 1)

        @block.sync
        def _(sp):
            for g in range(0, IMAGES, 4):
                sp.dma_start(x_all[:, g:g + 2], x_v[:, g:g + 2]).then_inc(s_x[g], 16)
            sp.dma_start(packed[W0][:, :], packs[W0][0]).then_inc(s_packed[W0], 16)
            for g in range(IMAGES):
                wait_drained(sp, "y", 3, g)
                sp.dma_start(out_v[g], y[g][:, :, :]).then_inc(s_y, 16)
            sp.wait_ge(s_y, 16 * IMAGES)

        @block.gpsimd
        def _(pool):
            nc.gpsimd.memset(neg_half[:, :], -0.5).then_inc(s_half, 1)
            pool.wait_ge(s_half, 1)
            for g in range(EARLY, IMAGES - LATE):
                clear_kdiag(nc.gpsimd, g)
            for n in range(2):
                wait_drained(pool, "group var", 0, n * HALF)
                at = slice(n * HALF, (n + 1) * HALF)
                nc.gpsimd.tensor_tensor(var_gn[:, at], var_gn[:, at], neg_half[:, :], ALU.pow).then_inc(s_rstd, 1)
            pool.wait_ge(s_packed[W12], 16)
            pool.wait_ge(s_packed[W0], 16)
            for w, gate in (("w1v", "gamma1"), ("w2v", "gamma2")):
                nc.gpsimd.tensor_scalar(part[w], part[w], part[gate], None, ALU.mult).then_inc(s_gated, 1)
            for g in range(IMAGES):
                nc.gpsimd.memset(windows[g], 0.0).then_inc(s_windows, 1)
            for step, layer, g in sequence:
                if step == "scale":
                    pool.wait_ge(s_inv, nth("scale", layer, g))
                    p = prob[g][:, 1, 0:keys_of(layer)]
                    nc.gpsimd.tensor_tensor(p, p, inv[g][:, 1, 0:1].broadcast_to([128, keys_of(layer)]), ALU.mult)\
                        .then_inc(s_scaled1, 1)
                if step == "setup":
                    for late in range(IMAGES - LATE, IMAGES):
                        clear_kdiag(nc.gpsimd, late)
                    for i in range(IMAGES // 2):
                        nc.gpsimd.memset(vdiag[i][:, :, :, :], 0.0).then_inc(s_zero, 1)
                if step == "share3":
                    pool.wait_ge(s_inv3, 2 * (g + 1))
                    for t in range(TILES):
                        p = view(prob[g][:, t, :], HEADS)
                        nc.gpsimd.tensor_tensor(p, p, inv[g][:, t, :].unsqueeze(2).broadcast_to([128, HEADS, KEYS]), ALU.mult)\
                            .then_inc(s_share3, 1)
                if step == "xb":
                    wait_filled(pool, "scores1", 3, g)
                    nc.gpsimd.tensor_scalar(xb[g], xT[g][:, :], part["bo3"], None, ALU.add).then_inc(s_xb, 1)
                if step == "pool":
                    wait_drained(pool, "o", 2, g)
                    xi = xT[g][:, :].rearrange("p (h w) -> p h w", w=SIDE)
                    w, p = poolW[g], poolT[g // 2][:, g % 2, :, :]
                    first = g * POOL_STEPS
                    nc.gpsimd.tensor_tensor(w[:, :, :], xi[:, :, 0::2], xi[:, :, 1::2], ALU.add).then_inc(s_pool, 1)
                    pool.wait_ge(s_pool, first + 1)
                    nc.gpsimd.tensor_tensor(w[:, :, 0:PSIDE - 1], w[:, :, 0:PSIDE - 1], xi[:, :, 2::2], ALU.add)\
                        .then_inc(s_pool, 1)
                    pool.wait_ge(s_pool, first + 2)
                    nc.gpsimd.tensor_tensor(p, w[:, 0::2, :], w[:, 1::2, :], ALU.add).then_inc(s_pool, 1)
                    pool.wait_ge(s_pool, first + 3)
                    nc.gpsimd.tensor_tensor(p[:, 0:PSIDE - 1, :], p[:, 0:PSIDE - 1, :], w[:, 2::2, :], ALU.add).then_inc(s_pool, 1)
                    pool.wait_ge(s_pool, first + 4)
                    nc.gpsimd.tensor_tensor(p, p, view(inv_count, PSIDE), ALU.mult).then_inc(s_pool, 1)

        @block.scalar
        def _(act):
            act.dma_start(packed[CONST_F][:, :], packs[CONST_F][0]).then_inc(s_packed[CONST_F], 16)
            for g in range(2, IMAGES, 4):
                act.dma_start(x_all[:, g:g + 2], x_v[:, g:g + 2]).then_inc(s_x[g], 16)
            act.dma_start(packed[W12][:, :], packs[W12][0]).then_inc(s_packed[W12], 16)
            act.dma_start(packed[CONST_B][:, :], packs[CONST_B][0]).then_inc(s_packed[CONST_B], 16)
            act.dma_start(packed[W3][:, :], packs[W3][0]).then_inc(s_packed[W3], 16)

            def normalise(g):
                act.wait_ge(s_factors, 2 * (g // HALF + 1))
                raw = view(psum("xT", 0, g - g % 2)[:, :], 2)[:, g % 2, :] if g < HALF else xT[g][:, :]
                nc.scalar.activation(xT[g][:, :], raw, ACT.Identity, bias=shift_gn[:, g:g + 1], scale=scale_gn[:, g:g + 1])\
                    .then_inc(*(drained_by("xT", 0, g - 1) if g < HALF and g % 2 else (s_normed, 1)))

            def values(layer, g):
                wait_filled(act, "v", layer, g)
                nc.scalar.activation(v[g][:, :, :], view(psum("v", layer, g)[:, 0:TOK], TILES), ACT.Copy)\
                    .then_inc(*drained_by("v", layer, g))

            def queries_keys(layer, g):
                wait_filled(act, "qk", layer, g)
                for n in range(2 * 2):
                    to, ps = qT[g + n // 2][0:DQK, n % 2, :], psum("qk", layer, g)[STRIP * n:STRIP * n + DQK, 0:TOK]
                    if layer == 1:
                        last = nc.scalar.activation(to, ps, ACT.Relu, bias=part[("bq1", "bk1")[n % 2]][0:DQK])
                    else:
                        last = nc.scalar.activation(to, ps, ACT.Copy)
                last.then_inc(*drained_by("qk", layer, g))

            def exponentials(layer, g):
                keys = keys_of(layer)
                act.wait_ge(s_max, nth("scores", layer, g))
                for t in range(TILES):
                    last = nc.scalar.activation(prob[g][:, t, 0:keys], psum("scores", layer, g)[:, keys * t:keys * t + keys],
                                                ACT.Exp, bias=negmax[g][:, t, 0:1], accum_out=total[g][:, t:t + 1])
                last.then_inc(*drained_by("scores", layer, g))

            def kv_strips(g):
                for k in range(2):
                    wait_drained(act, f"kv{k}", 3, g)
                    for b in range(DVE_STRIPS, STRIPS):
                        last = nc.scalar.activation(*kv_strip(g, k, b), ACT.Copy)
                last.then_inc(s_strips_act, 1)

            def queries3(g):
                wait_filled(act, "q", 3, g)
                for a in range(HALVES):
                    last = nc.scalar.activation(qT[g][:, a, :], psum("q", 3, g)[:, TOK * a:TOK * a + TOK], ACT.Identity,
                                                bias=part["bq3"][:, a:a + 1], scale=float(DH) ** -0.5)
                last.then_inc(*drained_by("q", 3, g))

            def values3(g):
                wait_filled(act, "vd", 3, g)
                ps = psum("vd", 3, g)[:, 0:2 * PAIRS * STRIP].rearrange("p (i e) -> p i e", e=STRIP)
                vd = vdiag[g // 2][:, :, :, :].rearrange("p (i two) c e -> p i two c e", two=2)
                for c2 in range(2):
                    for odd in range(2):
                        last = nc.scalar.activation(vd[KEYS * c2:KEYS * c2 + KEYS, :, odd, c2, :],
                                                    ps[KEYS * odd:KEYS * odd + KEYS, :, DH:], ACT.Copy)
                last.then_inc(*drained_by("vd", 3, g))

            act.wait_ge(s_packed[CONST_F], 16)
            nc.scalar.activation(warm[:, :], ident[:, 0:1], ACT.Exp)
            for g in range(HALF, IMAGES, 2):
                wait_filled(act, "xT", 0, g)
                for n in range(2):
                    last = nc.scalar.activation(xT[g + n][:, :], view(psum("xT", 0, g)[:, :], 2)[:, n, :], ACT.Copy)
                last.then_inc(*drained_by("xT", 0, g))
            for step, layer, g in sequence:
                if step == "norm":
                    normalise(g)
                if step == "qk" and layer > 0:
                    queries_keys(layer, g)
                if step == "v":
                    values(layer, g)
                if step == "scores":
                    exponentials(layer, g)
                if step == "probT":
                    wait_filled(act, "probT", layer, g)
                    keys = TILES * keys_of(layer)
                    nc.scalar.activation(probT[g][:, 0, 0:keys], psum("probT", layer, g)[:, 0:keys], ACT.Copy)\
                        .then_inc(*drained_by("probT", layer, g))
                if step == "kv":
                    if g == 0:
                        act.wait_ge(s_zero, IMAGES + IMAGES // 2)
                    kv_strips(g)
                if step == "q":
                    if g == 0:
                        act.wait_ge(s_bias, 2)
                    queries3(g)
                if step == "vd":
                    values3(g)
                if step == "scores3":
                    for t in range(TILES):
                        wait_drained(act, f"scores{t}", 3, g)
                        nc.scalar.activation(prob[g][:, t, :], prob[g][:, t, :], ACT.Exp).then_inc(s_exp3, 1)
                if step == "probT3":
                    for t in range(TILES):
                        wait_filled(act, f"probT{t}", 3, g)
                        nc.scalar.activation(probT[g][:, t, :], psum(f"probT{t}", 3, g)[:, :], ACT.Copy)\
                            .then_inc(*drained_by(f"probT{t}", 3, g))
                if step == "x":
                    wait_filled(act, "x", 3, g)
                    nc.scalar.activation(y[g], view(psum("x", 3, g)[:, 0:TOK], TILES), ACT.Copy).then_inc(*drained_by("x", 3, g))
                if step == "pv":
                    wait_filled(act, "pv", 3, g)
                    nc.scalar.activation(oT[g], psum("pv", 3, g)[:, 0:TOK], ACT.Copy).then_inc(*drained_by("pv", 3, g))

        @block.vector
        def _(dve):
            steps = [0]

            def link(ins):
                ins.then_inc(s_norm, 1)
                steps[0] += 1
                dve.wait_ge(s_norm, steps[0])

            def moments(g):
                (wait_filled if g < HALF else wait_drained)(dve, "xT", 0, g - g % 2)
                raw = view(psum("xT", 0, g - g % 2)[:, :], 2)[:, g % 2, :] if g < HALF else xT[g][:, :]
                nc.vector.bn_stats(stats[:, g, :, :], raw).then_inc(s_moments, 1)

            def deviations(g):
                at = slice(g, g + HALF)
                dve.wait_ge(s_moments, g + HALF)
                link(nc.vector.tensor_scalar(stats[:, at, :, 2], stats[:, at, :, 2], 2.0 / TOK, GN_EPS, ALU.mult, ALU.add))
                wait_filled(dve, "group mean", 0, g)
                link(nc.vector.tensor_reduce(out=means[:, at], in_=psum("group mean", 0, g)[:, 0:2 * HALF].rearrange(
                    "p (g h) -> p g h", h=2), op=ALU.add, axis=AX.X))
                link(nc.vector.tensor_tensor(spread[:, at, :], stats[:, at, :, 1],
                                             means[:, at].unsqueeze(2).broadcast_to([128, HALF, 2]), ALU.subtract))
                link(nc.vector.tensor_tensor(spread[:, at, :], spread[:, at, :], spread[:, at, :], ALU.mult))
                nc.vector.tensor_tensor(spread[:, at, :], spread[:, at, :], stats[:, at, :, 2], ALU.add)\
                    .then_inc(*drained_by("group mean", 0, g))

            def variances(g):
                at = slice(g, g + HALF)
                wait_filled(dve, "group var", 0, g)
                nc.vector.tensor_reduce(out=var_gn[:, at], in_=psum("group var", 0, g)[:, 0:2 * HALF].rearrange("p (g h) -> p g h", h=2),
                                        op=ALU.add, axis=AX.X).then_inc(*drained_by("group var", 0, g))
                dve.wait_ge(s_packed[W0], 16)
                link(nc.vector.tensor_scalar(means[:, at], means[:, at], -1.0, part["gn_gamma"], ALU.mult, ALU.mult))

            def factors(g):
                at = slice(g, g + HALF)
                dve.wait_ge(s_rstd, g // HALF + 1)
                nc.vector.tensor_scalar(scale_gn[:, at], var_gn[:, at], part["gn_gamma"], None, ALU.mult).then_inc(s_factors, 1)
                link(nc.vector.tensor_tensor(shift_gn[:, at], means[:, at], var_gn[:, at], ALU.mult))
                nc.vector.tensor_scalar(shift_gn[:, at], shift_gn[:, at], part["gn_beta"], None, ALU.add).then_inc(s_factors, 1)

            def prepare():
                nc.vector.tensor_scalar(part["bv1"], part["bv1"], part["gamma1"], None, ALU.mult).then_inc(s_bias, 1)
                nc.vector.tensor_scalar(part["bq3"], part["bq3"], float(DH) ** -0.5, None, ALU.mult).then_inc(s_bias, 1)
                dve.wait_ge(s_bias, 2)

            def queries_keys0(g):
                wait_filled(dve, "qk", 0, g)
                ps = psum("qk", 0, g)
                nc.vector.tensor_scalar(qT[g][:, 0, :], ps[:, 0:TOK], part["bq0"], float(C) ** -0.5, ALU.add, ALU.mult)
                nc.vector.tensor_scalar(qT[g][:, 1, :], ps[:, TOK:], part["bk0"], None, ALU.add).then_inc(*drained_by("qk", 0, g))

            def maxima(layer, g):
                wait_filled(dve, "scores", layer, g)
                nc.vector.tensor_reduce(out=negmax[g][:, :, 0], in_=view(psum("scores", layer, g)[:, 0:TILES * keys_of(layer)], TILES),
                                        op=ALU.max, axis=AX.X, negate=True).then_inc(s_max, 1)

            def scale_prob(layer, g):
                wait_drained(dve, "scores", layer, g)
                nc.vector.reciprocal(inv[g][:, :, 0], total[g][:, :]).then_inc(s_inv, 1)
                dve.wait_ge(s_inv, nth("scale", layer, g))
                p = prob[g][:, 0, 0:keys_of(layer)]
                nc.vector.tensor_scalar(p, p, inv[g][:, 0, 0:1], None, ALU.mult).then_inc(s_scaled0, 1)

            def turn_windows(g):
                wait_drained(dve, "scores", 1, g)
                nc.vector.reciprocal(inv[g][:, :, 0], total[g][:, :]).then_inc(s_turn, 1)
                dve.wait_ge(s_turn, TURN_STEPS * g + 1)
                p = prob[g][:, :, 0:STRIP]
                nc.vector.tensor_tensor(p, p, inv[g][:, :, 0:1].broadcast_to([128, TILES, STRIP]), ALU.mult).then_inc(s_turn, 1)
                dve.wait_ge(s_turn, TURN_STEPS * g + 2)
                dve.wait_ge(s_windows, g + 1)
                for s in range(STRIPS):
                    at = slice(STRIP * s, STRIP * s + STRIP)
                    last = nc.vector.transpose(windows[g][at, :, at], p[at])
                last.then_inc(s_turn, 1)

            def update(layer, g):
                wait_filled(dve, "o", layer, g)
                ps = psum("o", layer, g)[:, 0:TOK]
                if layer < 2:
                    last = nc.vector.scalar_tensor_tensor(out=xT[g][:, :], in0=ps, scalar=part[("bv0", "bv1")[layer]],
                                                          in1=xT[g][:, :], op0=ALU.add, op1=ALU.add)
                else:
                    last = nc.vector.tensor_tensor(xT[g][:, :], ps, xT[g][:, :], ALU.add)
                last.then_inc(*drained_by("o", layer, g))

            def scores3(g, t):
                wait_filled(dve, f"scores{t}", 3, g)
                s3 = view(psum(f"scores{t}", 3, g)[:, :], HEADS)
                nc.vector.tensor_reduce(out=negmax[g][:, t, :], in_=s3, op=ALU.max, axis=AX.X, negate=True).then_inc(s_max3, 1)
                dve.wait_ge(s_max3, TILES * g + t + 1)
                nc.vector.tensor_tensor(view(prob[g][:, t, :], HEADS), s3,
                                        negmax[g][:, t, :].unsqueeze(2).broadcast_to([128, HEADS, KEYS]), ALU.add)\
                    .then_inc(*drained_by(f"scores{t}", 3, g))

            def sums3(g):
                dve.wait_ge(s_exp3, TILES * (g + 1))
                nc.vector.tensor_reduce(out=inv[g][:, :, :], in_=prob[g][:, :, :].rearrange("p t (c m) -> p t c m", c=HEADS),
                                        op=ALU.add, axis=AX.X).then_inc(s_inv3, 1)
                dve.wait_ge(s_inv3, 2 * g + 1)
                nc.vector.reciprocal(inv[g][:, :, :], inv[g][:, :, :]).then_inc(s_inv3, 1)

            nc.vector.memset(warm_up[:, :], 0.0).then_inc(s_warm, 1)
            for g in range(EARLY):
                clear_kdiag(nc.vector, g)
            for g in range(HALF):
                moments(g)
            deviations(0)
            moments(HALF)
            variances(0)
            moments(HALF + 1)
            moments(HALF + 2)
            factors(0)
            moments(HALF + 3)
            deviations(HALF)
            variances(HALF)
            factors(HALF)
            for step, layer, g in sequence:
                if step == "qk" and layer == 0:
                    queries_keys0(g)
                if step == "setup":
                    prepare()
                if step == "scores":
                    maxima(layer, g)
                if step == "scale":
                    scale_prob(layer, g)
                if step == "turn":
                    turn_windows(g)
                if step == "o":
                    update(layer, g)
                if step == "kv":
                    if g == 0:
                        dve.wait_ge(s_packed[W3], 16)
                        dve.wait_ge(s_zero, IMAGES + IMAGES // 2)
                    half = HEADS // 2
                    for k in range(2):
                        wait_filled(dve, f"kv{k}", 3, g)
                        bias = part["bkv3"][:, half * k:half * k + half].unsqueeze(2).broadcast_to([128, half, 2 * PTOK])
                        nc.vector.tensor_tensor(view(prob[g + k][:, 1, :], half), view(psum(f"kv{k}", 3, g)[:, :], half), bias,
                                                ALU.add).then_inc(*drained_by(f"kv{k}", 3, g))
                    for k in range(2):
                        wait_drained(dve, f"kv{k}", 3, g)
                        for b in range(DVE_STRIPS):
                            last = nc.vector.tensor_copy(*kv_strip(g, k, b))
                    last.then_inc(s_strips, 1)
                if step == "scores3":
                    for t in range(TILES):
                        scores3(g, t)
                if step == "share3":
                    sums3(g)
                if step == "y":
                    wait_filled(dve, "y", 3, g)
                    wait_drained(dve, "x", 3, g)
                    nc.vector.tensor_tensor(y[g], view(psum("y", 3, g)[:, 0:TOK], TILES), y[g], ALU.add)\
                        .then_inc(*drained_by("y", 3, g))

        @block.tensor
        def _(pe):
            mm, transpose = nc.tensor.matmul, nc.tensor.transpose

            def begin(kind, layer, g=0):
                b, n = place[kind, layer, g] % BANKS, count(kind, layer, g)
                if n > 1:
                    pe.wait_ge(drained[b], n - 1)
                return bank[b]

            def averages(kind, g, of):
                mm(begin(kind, 0, g)[:, 0:2 * HALF], group_avg, of, start=True, stop=True).then_inc(*filled_by(kind, 0, g))

            def image_ready(layer, g):
                if layer == 0 and g < HALF and g % 2:
                    wait_drained(pe, "xT", 0, g - 1)
                elif layer == 0:
                    pe.wait_ge(s_normed, g // 2 + 1 if g < HALF else g - HALF // 2 + 1)
                else:
                    wait_drained(pe, "o", layer - 1, g)

            def project(layer, g):
                image_ready(layer, g)
                ps = begin("qk", layer, g)
                if layer == 0:
                    mm(ps[:, 0:TOK], part["w0q"], xT[g][:, :], start=True, stop=True)
                    last = mm(ps[:, TOK:], part["w0k"], xT[g][:, :], start=True, stop=True)
                else:
                    image_ready(layer, g + 1)
                    for n in range(2 * 2):
                        last = mm(ps[STRIP * n:STRIP * n + STRIP, 0:TOK], part[f"w{layer}" + "qk"[n % 2]], xT[g + n // 2][:, :],
                                  start=True, stop=True)
                last.then_inc(*filled_by("qk", layer, g))

            def values(layer, g):
                image_ready(layer, g)
                ps = begin("v", layer, g)
                for t in range(TILES):
                    last = mm(ps[:, C * t:C * t + C], xT[g][:, 128 * t:128 * t + 128], part[f"w{layer}v"], start=True, stop=True)
                last.then_inc(*filled_by("v", layer, g))

            def score(layer, g):
                wait_drained(pe, "qk", layer, g if layer == 0 else g - g % 2)
                q, k = (qT[g][0:C if layer == 0 else DQK, n, :] for n in range(2))
                ps = begin("scores", layer, g)
                if layer == 1:
                    mm(ps[:, 0:TILES * STRIP], mask_l, mask_r, start=True, stop=False, skip_group_check=True)
                for t in range(TILES):
                    at = slice(128 * t, 128 * t + 128)
                    if layer == 1:
                        for s in range(STRIPS):
                            rows = slice(128 * t + STRIP * s, 128 * t + STRIP * s + STRIP)
                            last = mm(ps[STRIP * s:STRIP * s + STRIP, STRIP * t:STRIP * t + STRIP], q[:, rows], k[:, rows],
                                      start=False, stop=t == TILES - 1, skip_group_check=True)
                    else:
                        last = mm(ps[:, TOK * t:TOK * t + TOK], q[:, at], k, start=True, stop=True)
                last.then_inc(*filled_by("scores", layer, g))

            def turn_prob(layer, g):
                ps = begin("probT", layer, g)
                for t, scaled in enumerate((s_scaled0, s_scaled1)):
                    pe.wait_ge(scaled, nth("scale", layer, g))
                    for k in range(keys_of(layer) // 128):
                        last = transpose(ps[:, TOK * k + 128 * t:TOK * k + 128 * t + 128], prob[g][:, t, 128 * k:128 * k + 128], ident)
                last.then_inc(*filled_by("probT", layer, g))

            def apply(layer, g):
                wait_drained(pe, "v", layer, g)
                if layer == 1:
                    pe.wait_ge(s_turn, TURN_STEPS * (g + 1))
                else:
                    wait_drained(pe, "probT", layer, g)
                vals = v[g]
                ps = begin("o", layer, g)
                for k in range(TILES):
                    if layer == 1:
                        last = mm(ps[:, 128 * k:128 * k + 128], vals[:, k, :], windows[g][:, k, :],
                                  start=True, stop=True)
                    else:
                        last = mm(ps[:, 0:TOK], vals[:, k, :], probT[g][:, 0, TOK * k:TOK * k + TOK], start=k == 0, stop=k == TILES - 1)
                last.then_inc(*filled_by("o", layer, g))

            def keys_values3(g):
                pe.wait_ge(s_pool, (g + 2) * POOL_STEPS)
                half = HEADS // 2
                for k in range(2):
                    ps = begin(f"kv{k}", 3, g)
                    for c in range(half * k, half * k + half):
                        at = 128 * (c % half)
                        last = mm(ps[:, at:at + 2 * PTOK], part["w3kv"][:, 128 * c:128 * c + 128],
                                  poolT[g // 2][:, :, :, :].rearrange("p i h w -> p (i h w)"), start=True, stop=True)
                    last.then_inc(*filled_by(f"kv{k}", 3, g))

            def queries3(g):
                ps = begin("q", 3, g)
                for a in range(HALVES):
                    last = mm(ps[:, TOK * a:TOK * a + TOK], part["w3q"][:, 128 * a:128 * a + 128], xT[g][:, :], start=True, stop=True)
                last.then_inc(*filled_by("q", 3, g))

            def turn_values3(g):
                pe.wait_ge(s_strips, g // 2 + 1)
                ps = begin("vd", 3, g)
                for i in range(2 * PAIRS):
                    last = transpose(ps[:, STRIP * i:STRIP * i + STRIP], kdiag[g // 2][0:STRIP, 0, 128 * i:128 * i + 128],
                                     ident[0:STRIP, 0:STRIP])
                last.then_inc(*filled_by("vd", 3, g))

            def score3(g, t):
                wait_drained(pe, "q", 3, g)
                pe.wait_ge(s_strips, g // 2 + 1)
                pe.wait_ge(s_strips_act, g // 2 + 1)
                ps = begin(f"scores{t}", 3, g)
                for a in range(HALVES):
                    for s in range(STRIPS):
                        j = STRIPS * t + s
                        key = KEYS * (HEADS * (g % 2) + j)
                        last = mm(view(ps[STRIP * s:STRIP * s + STRIP, TOK * a:TOK * a + TOK], STRIPS),
                                  qT[g][:, a, HTOK * j:HTOK * j + HTOK], kdiag[g // 2][:, :, key:key + KEYS], start=True, stop=True)
                last.then_inc(*filled_by(f"scores{t}", 3, g))

            def turn_prob3(g, t):
                pe.wait_ge(s_share3, TILES * g + t + 1)
                ps = begin(f"probT{t}", 3, g)
                for p in range(PAIRS):
                    last = transpose(ps[:, 128 * p:128 * p + 128], prob[g][:, t, 128 * p:128 * p + 128], ident)
                last.then_inc(*filled_by(f"probT{t}", 3, g))

            def apply3(g):
                wait_drained(pe, "vd", 3, g - g % 2)
                ps = begin("pv", 3, g)
                for t in range(TILES):
                    wait_drained(pe, f"probT{t}", 3, g)
                    for p in range(PAIRS):
                        for s in range(STRIPS):
                            at, j = HTOK * (STRIPS * t + s), STRIPS * t + s
                            last = mm(ps[STRIP * p:STRIP * p + STRIP, at:at + HTOK],
                                      vdiag[g // 2][:, HEADS * (g % 2) + j, :, :].rearrange("p c e -> p (c e)"),
                                      probT[g][:, t, 128 * p + STRIP * s:128 * p + STRIP * s + STRIP], start=True, stop=True)
                last.then_inc(*filled_by("pv", 3, g))

            def turn_back(g):
                pe.wait_ge(s_xb, g + 1)
                ps = begin("x", 3, g)
                for t in range(TILES):
                    last = transpose(ps[:, C * t:C * t + C], xb[g][:, 128 * t:128 * t + 128], ident)
                last.then_inc(*filled_by("x", 3, g))

            def out3(g):
                wait_drained(pe, "pv", 3, g)
                ps = begin("y", 3, g)
                for t in range(TILES):
                    last = mm(ps[:, C * t:C * t + C], oT[g][:, 128 * t:128 * t + 128], part["w3o"], start=True, stop=True)
                last.then_inc(*filled_by("y", 3, g))

            def turn_images(g):
                pe.wait_ge(s_x[g], 16)
                ps = begin("xT", 0, g)
                for n in range(2 * TILES):
                    last = transpose(ps[:, 128 * n:128 * n + 128], x_in[g + n // TILES][:, n % TILES, :], ident)
                last.then_inc(*filled_by("xT", 0, g))

            def group_means(g):
                pe.wait_ge(s_moments, g + HALF)
                averages("group mean", g, stats[:, g:g + HALF, :, 1])

            def group_variances(g):
                wait_drained(pe, "group mean", 0, g)
                averages("group var", g, spread[:, g:g + HALF, :])

            def keep_warm(times):
                for _ in range(times):
                    mm(bank[BANKS - 1][:, 0:TOK], warm_up[:, 0:128], warm_up[:, :], start=True, stop=True)

            FIRST = 13
            AFTER = (2, 2, 2, 8, 4)
            pe.wait_ge(s_warm, 1)
            keep_warm(FIRST)
            pe.wait_ge(s_packed[CONST_F], 16)
            turn_images(0)
            keep_warm(AFTER[0])
            turn_images(2)
            turn_images(4)
            keep_warm(AFTER[1])
            group_means(0)
            turn_images(6)
            keep_warm(AFTER[2])
            group_variances(0)
            keep_warm(AFTER[3])
            group_means(HALF)
            keep_warm(AFTER[4])
            pe.wait_ge(s_packed[W0], 16)
            for step, layer, g in sequence:
                if step == "qk":
                    if layer == 1 and g == 0:
                        pe.wait_ge(s_packed[W12], 16)
                        pe.wait_ge(s_gated, 2)
                    project(layer, g)
                if step == "group var":
                    group_variances(g)
                if step == "v":
                    values(layer, g)
                if step == "scores":
                    if layer == 1 and g == 0:
                        pe.wait_ge(s_packed[CONST_B], 16)
                    score(layer, g)
                if step == "probT":
                    turn_prob(layer, g)
                if step == "o":
                    apply(layer, g)
                if step in ("q", "kv") and g == 0:
                    pe.wait_ge(s_packed[W3], 16)
                if step == "kv":
                    keys_values3(g)
                if step == "q":
                    queries3(g)
                if step == "vd":
                    turn_values3(g)
                if step == "scores3":
                    for t in range(TILES):
                        score3(g, t)
                if step == "probT3":
                    for t in range(TILES):
                        turn_prob3(g, t)
                if step == "pv":
                    apply3(g)
                if step == "x":
                    turn_back(g)
                if step == "y":
                    out3(g)


def kernel(**inputs):
    import numpy as _np
    import ml_dtypes as _mld
    import concourse.bacc as _bacc
    from concourse import mybir as _mybir
    from concourse.bass_utils import run_bass_kernel_spmd as _run

    nc = _bacc.Bacc("TRN2", target_bir_lowering=False, num_devices=1)
    inputs = {k: _np.asarray(v) for k, v in inputs.items()}
    arrays = {"in_x_dram": _np.ascontiguousarray(inputs["x"])}
    groups = [*constants(), *arrange(inputs)]
    packs = []
    for n, group in enumerate(groups):
        where, at = {}, 0
        for name, a in group.items():
            where[name] = (at, at + a.shape[1])
            at += a.shape[1]
        a = _np.ascontiguousarray(_np.concatenate(list(group.values()), axis=1))
        if n == 1:
            a = a.astype(_mld.bfloat16)
        arrays[f"in_pack{n}_dram"] = a
        packs.append((nc.dram_tensor(f"in_pack{n}_dram", a.shape, _mybir.dt.from_np(a.dtype), kind="ExternalInput").ap(), where))
    x = nc.dram_tensor("in_x_dram", inputs["x"].shape, _mybir.dt.float32, kind="ExternalInput").ap()
    out = nc.dram_tensor("out_0_dram", (IMAGES, SIDE, SIDE, C), _mybir.dt.float32, kind="ExternalOutput").ap()
    build(nc, x, packs, out)
    r = _run(nc, [arrays], core_ids=[0])
    return r.results[0]["out_0_dram"]
```
